# Optimizing a Trainium2 kernel written in Bass

```python
import numpy as np
import jax
import jax.numpy as jnp

def _softmax(x, axis=-1):
    return jax.nn.softmax(x, axis=axis)

def _gelu(x):
    return jax.nn.gelu(x, approximate=True)

def _silu(x):
    return jax.nn.silu(x)

def _sigmoid(x):
    return jax.nn.sigmoid(x)

def _layernorm(x, axis=-1, eps=1e-05):
    m = jnp.mean(x, axis=axis, keepdims=True)
    v = jnp.var(x, axis=axis, keepdims=True)
    return (x - m) / jnp.sqrt(v + eps)

def _scatter_add(tgt, idx, src, axis=0):
    return tgt.at[idx].add(src)

def _segment_sum(src, seg, n):
    return jax.ops.segment_sum(src, seg, n)
kernel_name = 'mk_conv_attn_hybrid_d2_conv_nchw512_r4_565495'

def setup_inputs(seed: int=0):
    np.random.seed(seed)
    _w = jnp.asarray

    def _rec_inputs():
        import jax
        import jax.numpy as jnp
        _gk = jax.random.key(seed)
        x = -0.0003929 + 0.9999 * jax.random.normal(jax.random.fold_in(_gk, 1), (8, 128, 16, 16), jnp.float32)
        return x
    x = _rec_inputs()

    def _L0_conv_setup():
        import jax, jax.numpy as jnp
        import numpy as np
        import math
        B, C, P, H, W = (8, 128, 64, 16, 16)
        key = jax.random.key(seed)
        ks = jax.random.split(key, 6)
        x = jax.random.normal(ks[0], (B, C, H, W), dtype=jnp.float32)
        wq = jax.random.normal(ks[1], (P, C), dtype=jnp.float32) * 0.01
        bq = jnp.zeros((P,), dtype=jnp.float32)
        wk = jax.random.normal(ks[2], (P, C), dtype=jnp.float32) * 0.01
        bk = jnp.zeros((P,), dtype=jnp.float32)
        wv = jax.random.normal(ks[3], (C, C), dtype=jnp.float32) * 0.01
        wkm = jax.random.normal(ks[4], (1, C), dtype=jnp.float32) * 0.01
        bkm = jnp.zeros((1,), dtype=jnp.float32)
        gamma = jax.random.normal(ks[5], (1,), dtype=jnp.float32)
        return {'x': x, 'wq': wq, 'bq': bq, 'wk': wk, 'bk': bk, 'wv': wv, 'wkm': wkm, 'bkm': bkm, 'gamma': gamma}
    _L0_conv_all = _L0_conv_setup()
    _L0_conv_in = {k: v for k, v in _L0_conv_all.items() if k in ('wq', 'bq', 'wk', 'bk', 'wv', 'wkm', 'bkm', 'gamma')}
    del _L0_conv_all

    def _L1_attn_setup():
        import jax, jax.numpy as jnp
        import numpy as np
        NUM_HEADS = 8
        EPS = 1e-06
        WSCALE = 0.02
        key = jax.random.key(seed)
        ks = jax.random.split(key, 5)
        L, N, E = (256, 2, 128)
        inp = {'query': jax.random.normal(ks[0], (L, N, E), dtype=jnp.float32)}
        for i, name in enumerate(['q', 'k', 'v', 'out']):
            inp[name + '_w'] = jax.random.normal(ks[i + 1], (E, E), dtype=jnp.float32) * WSCALE
            inp[name + '_b'] = jnp.zeros((E,), dtype=jnp.float32)
        return inp
    _L1_attn_all = _L1_attn_setup()
    _L1_attn_in = {k: v for k, v in _L1_attn_all.items() if k in ('q_w', 'q_b', 'k_w', 'k_b', 'v_w', 'v_b', 'out_w', 'out_b')}
    del _L1_attn_all

    def _L1_ffn_setup():
        import jax, jax.numpy as jnp
        import numpy as np
        TOP_K = 2
        key = jax.random.key(seed)
        k0, k1, k2, k3, k4 = jax.random.split(key, 5)
        B, S, D, F, E = (1, 512, 128, 256, 8)
        scale = 0.02
        hidden_states = jax.random.normal(k0, (B, S, D), dtype=jnp.float32)
        router_w = jax.random.normal(k1, (D, E), dtype=jnp.float32) * scale
        w1 = jax.random.normal(k2, (E, D, F), dtype=jnp.float32) * scale
        w2 = jax.random.normal(k3, (E, F, D), dtype=jnp.float32) * scale
        w3 = jax.random.normal(k4, (E, D, F), dtype=jnp.float32) * scale
        return {'hidden_states': hidden_states, 'router_w': router_w, 'w1': w1, 'w2': w2, 'w3': w3}
    _L1_ffn_all = _L1_ffn_setup()
    _L1_ffn_in = {k: v for k, v in _L1_ffn_all.items() if k in ('router_w', 'w1', 'w2', 'w3')}
    del _L1_ffn_all
    return {'x': x, 'L0_conv_wq': _L0_conv_in['wq'], 'L0_conv_bq': _L0_conv_in['bq'], 'L0_conv_wk': _L0_conv_in['wk'], 'L0_conv_bk': _L0_conv_in['bk'], 'L0_conv_wv': _L0_conv_in['wv'], 'L0_conv_wkm': _L0_conv_in['wkm'], 'L0_conv_bkm': _L0_conv_in['bkm'], 'L0_conv_gamma': _L0_conv_in['gamma'], 'L1_attn_q_w': _L1_attn_in['q_w'], 'L1_attn_q_b': _L1_attn_in['q_b'], 'L1_attn_k_w': _L1_attn_in['k_w'], 'L1_attn_k_b': _L1_attn_in['k_b'], 'L1_attn_v_w': _L1_attn_in['v_w'], 'L1_attn_v_b': _L1_attn_in['v_b'], 'L1_attn_out_w': _L1_attn_in['out_w'], 'L1_attn_out_b': _L1_attn_in['out_b'], 'L1_ffn_router_w': _L1_ffn_in['router_w'], 'L1_ffn_w1': _L1_ffn_in['w1'], 'L1_ffn_w2': _L1_ffn_in['w2'], 'L1_ffn_w3': _L1_ffn_in['w3']}

def reference(x, L0_conv_wq, L0_conv_bq, L0_conv_wk, L0_conv_bk, L0_conv_wv, L0_conv_wkm, L0_conv_bkm, L0_conv_gamma, L1_attn_q_w, L1_attn_q_b, L1_attn_k_w, L1_attn_k_b, L1_attn_v_w, L1_attn_v_b, L1_attn_out_w, L1_attn_out_b, L1_ffn_router_w, L1_ffn_w1, L1_ffn_w2, L1_ffn_w3):
    import jax
    import jax.numpy as jnp

    def _L0_conv_ref(x, wq, bq, wk, bk, wv, wkm, bkm, gamma):
        import jax, jax.numpy as jnp
        import numpy as np
        import math
        B, C, P, H, W = (8, 128, 64, 16, 16)
        b, c, h, w = x.shape
        n = h * w
        xf = x.reshape(b, c, n)
        q = jnp.einsum('pc,bcn->bpn', wq, xf) + bq[None, :, None]
        k = jnp.einsum('pc,bcn->bpn', wk, xf) + bk[None, :, None]
        v = jnp.einsum('oc,bcn->bon', wv, xf)
        key_mask = jnp.einsum('c,bcn->bn', wkm[0], xf) + bkm
        scale = math.sqrt(q.shape[1])
        sim = jnp.einsum('bpm,bpn->bmn', q, k) / scale
        sim = sim + key_mask[:, None, :]
        sim = jax.nn.softmax(sim, axis=2)
        out = jnp.einsum('bmn,bcn->bcm', sim, v)
        out = out.reshape(b, c, h, w)
        return x + gamma[0] * out

    def _L1_attn_ref(query, q_w, q_b, k_w, k_b, v_w, v_b, out_w, out_b):
        import jax, jax.numpy as jnp
        import numpy as np
        NUM_HEADS = 8
        EPS = 1e-06
        WSCALE = 0.02
        L, N, E = query.shape
        H = NUM_HEADS
        d = E // H
        q = jax.nn.relu(query @ q_w.T + q_b)
        k = jax.nn.relu(query @ k_w.T + k_b)
        v = query @ v_w.T + v_b

        def split_heads(x):
            return x.reshape(L, N * H, d).transpose(1, 0, 2)
        q, k, v = (split_heads(q), split_heads(k), split_heads(v))
        theta = jnp.pi / 2 * jnp.arange(1, L + 1, dtype=query.dtype) / L
        s = jnp.sin(theta)[None, :, None]
        c = jnp.cos(theta)[None, :, None]
        q_ = jnp.concatenate([q * s, q * c], axis=-1)
        k_ = jnp.concatenate([k * s, k * c], axis=-1)
        kv = jnp.einsum('nld,nlm->nldm', k_, v)
        kv_cum = jnp.cumsum(kv, axis=1)
        qkv = jnp.einsum('nld,nldm->nlm', q_, kv_cum)
        k_cum = jnp.cumsum(k_, axis=1)
        denom = jnp.maximum(jnp.einsum('nld,nld->nl', q_, k_cum), EPS)
        attn = qkv / denom[..., None]
        attn = attn.transpose(1, 0, 2).reshape(L, N, E)
        return attn @ out_w.T + out_b

    def _L1_ffn_ref(hidden_states, router_w, w1, w2, w3):
        import jax, jax.numpy as jnp
        import numpy as np
        TOP_K = 2
        B, S, D = hidden_states.shape
        E = router_w.shape[1]
        x = hidden_states.reshape(-1, D)
        T = x.shape[0]
        router_logits = x @ router_w
        probs = jax.nn.softmax(router_logits.astype(jnp.float32), axis=-1)
        routing_weights, selected_experts = jax.lax.top_k(probs, TOP_K)
        routing_weights = routing_weights / routing_weights.sum(axis=-1, keepdims=True)
        routing_weights = routing_weights.astype(x.dtype)
        combine = jnp.zeros((T, E), dtype=x.dtype).at[jnp.arange(T)[:, None], selected_experts].add(routing_weights)
        gate = jax.nn.silu(jnp.einsum('td,edf->tef', x, w1))
        up = jnp.einsum('td,edf->tef', x, w3)
        h = gate * up * combine[:, :, None]
        out = jnp.einsum('tef,efd->td', h, w2)
        return out.reshape(B, S, D)

    def _gn(v, G=32, eps=1e-05):
        B_, C_, H_, W_ = v.shape
        g = v.reshape(B_, G, C_ // G, H_, W_)
        m = jnp.mean(g, axis=(2, 3, 4), keepdims=True)
        s = jnp.var(g, axis=(2, 3, 4), keepdims=True)
        return ((g - m) / jnp.sqrt(s + eps)).reshape(v.shape)

    def _ln_c(v, eps=1e-06):
        m = jnp.mean(v, axis=1, keepdims=True)
        s = jnp.var(v, axis=1, keepdims=True)
        return (v - m) / jnp.sqrt(s + eps)

    def _ln_t(v, eps=1e-05):
        m = jnp.mean(v, axis=-1, keepdims=True)
        s = jnp.var(v, axis=-1, keepdims=True)
        return (v - m) / jnp.sqrt(s + eps)

    def _to_tokens(v):
        B_, C_, H_, W_ = v.shape
        return v.reshape(B_, C_, H_ * W_).transpose(0, 2, 1)

    def _from_tokens(t, like):
        B_, C_, H_, W_ = like.shape
        return t.transpose(0, 2, 1).reshape(B_, C_, H_, W_)
    x = _L0_conv_ref(x, L0_conv_wq, L0_conv_bq, L0_conv_wk, L0_conv_bk, L0_conv_wv, L0_conv_wkm, L0_conv_bkm, L0_conv_gamma)
    t = _to_tokens(x)
    t = t + _L1_attn_ref(_ln_t(t), L1_attn_q_w, L1_attn_q_b, L1_attn_k_w, L1_attn_k_b, L1_attn_v_w, L1_attn_v_b, L1_attn_out_w, L1_attn_out_b)
    t = t + _L1_ffn_ref(_ln_t(t), L1_ffn_router_w, L1_ffn_w1, L1_ffn_w2, L1_ffn_w3)
    x = _from_tokens(t, x)
    return x

_drawn_inputs = setup_inputs


def setup_inputs(seed=0):
    import zlib

    import numpy as np

    out = dict(_drawn_inputs(seed))
    spreads = {'L0_conv_bq': (0.0, 0.8),
     'L0_conv_bk': (0.0, 0.8),
     'L1_attn_q_b': (0.0, 0.8),
     'L1_attn_k_b': (0.0, 0.8),
     'L1_attn_v_b': (0.0, 0.314),
     'L1_attn_out_b': (0.0, 0.1)}
    factors = {'L0_conv_wq': 8.0,
     'L0_conv_wk': 8.0,
     'L0_conv_wv': 8.0,
     'L0_conv_wkm': 8.0,
     'L1_attn_q_w': 5.366,
     'L1_attn_k_w': 4.355,
     'L1_ffn_router_w': 8.0,
     'L1_ffn_w1': 8.0,
     'L1_ffn_w2': 8.0,
     'L1_ffn_w3': 8.0}
    for name, (base, spread) in spreads.items():
        noise = np.random.default_rng([zlib.crc32(name.encode()), seed]).standard_normal(out[name].shape)
        drawn = base * np.exp(spread * noise) if base else spread * noise
        out[name] = jnp.asarray(drawn.astype(out[name].dtype))
    for name, factor in factors.items():
        out[name] = (out[name] * factor).astype(out[name].dtype)
    return out
```

```python
from contextlib import ExitStack

import numpy as np

import concourse.bass as bass
from concourse import mybir

ALU = mybir.AluOpType
ACT = mybir.ActivationFunctionType
AX = mybir.AxisListType
F32 = mybir.dt.float32
BF16 = mybir.dt.bfloat16
I32 = mybir.dt.int32
U32 = mybir.dt.uint32

P = 128
B = 8
N = 256
T = N // P
NT = B * T
TOKENS = B * N
PROJ = 64
H = 8
D = P // H
E = 8
F = 256
FK = F // P
TOP_K = 2
LN_EPS = 1e-5
DEN_EPS = 1e-6

CAP = TOKENS + P
DUMMY = E * CAP
BLOCKS = TOP_K * TOKENS // P + E - 1
ROW = P + 2
W_COL, DEST_COL = P, P + 1
SKIP = 1 << 20
UNROLL = 3
TURNS = BLOCKS // UNROLL
assert BLOCKS % UNROLL == 0
PARTS = 4

C_ID = 0
C_COS = C_ID + P
C_EXPERT = C_COS + B * H
C_ECAP = C_EXPERT + E
C_HALF = C_ECAP + E
C_BLOCK = C_HALF + T
C_END = C_BLOCK + BLOCKS

V_QB, V_KB, V_CQB, V_CKB, V_GAMMA, V_END = range(6)

T_ROW, T_EXPERT, T_PAD = 0, BLOCKS, 2 * BLOCKS
T_END = T_PAD + E


def constants():
    f = np.zeros((P, C_END), np.float32)
    f[:, C_ID:C_ID + P] = np.eye(P)
    for gap in range(B):
        for h in range(H):
            f[h * D:(h + 1) * D, C_COS + gap * H + h] = np.cos(np.pi / 2 * gap / B)
    f[:, C_EXPERT:C_EXPERT + E] = np.arange(E)
    f[:, C_ECAP:C_ECAP + E] = np.arange(E) * CAP
    f[:, C_HALF:C_HALF + T] = -0.5
    f[:, C_BLOCK:C_BLOCK + BLOCKS] = np.arange(BLOCKS)
    before = np.triu(np.ones((P, P), np.float32), 1)
    both = np.concatenate([before, np.ones((P, P), np.float32)], axis=1)
    dest = (np.arange(TOP_K)[None, None, :] * TOKENS + np.arange(P)[:, None, None] * NT
            + np.arange(NT)[None, :, None])
    return f, both, dest.reshape(P, NT * TOP_K).astype(np.float32)


def hybrid_block(nc, x_ch, x_tok, w_conv, w_lin, w_router, w13, w2, vecs, bias_rows, cst_f, cst_tri, cst_dest,
                 out):
    ctx = ExitStack()
    with ctx:
        def sb(name, shape, dt=F32):
            return ctx.enter_context(nc.sbuf_tensor(name, shape, dt))

        def sem(name):
            return ctx.enter_context(nc.semaphore(name))

        rows_x = nc.dram_tensor("rows_x", [E * CAP + P, ROW], F32, kind="Internal").ap()
        rows_y = nc.dram_tensor("rows_y", [TOP_K * TOKENS, P], F32, kind="Internal").ap()

        X = sb("X", [P, B, N])
        XT = sb("XT", [P, B, T, P])
        WC = sb("WC", [P, 2 * (PROJ + 1) + P])
        WL = sb("WL", [P, 4 * P])
        WR = sb("WR", [P, E])
        W13 = sb("W13", [P, E * 2 * F])
        W2 = sb("W2", [P, E * FK * P])
        VEC = sb("VEC", [P, V_END])
        BR = sb("BR", [65, 2 * P])
        CF = sb("CF", [P, C_END])
        TRI32 = sb("TRI32", [P, 2 * P])
        TRI = sb("TRI", [P, 2 * P], BF16)
        DEST = sb("DEST", [P, NT * TOP_K])
        wq, wk, wv = WC[:, 0:PROJ + 1], WC[:, PROJ + 1:2 * PROJ + 2], WC[:, 2 * PROJ + 2:]
        lq, lk, lv, lo = (WL[:, n * P:(n + 1) * P] for n in range(4))
        ident = CF[:, C_ID:C_ID + P]

        b_part = [sb(f"b_part{n}", [65, 2 * P], BF16) for n in range(3)]
        b_rest = [sb(f"b_rest{n}", [65, 2 * P]) for n in range(2)]
        BIAS = sb("BIAS", [65, 2 * P], BF16)
        ONES = sb("ONES", [65, P], BF16)
        vb_row, ob_row = BIAS[:, 0:P], BIAS[:, P:2 * P]
        cqb8 = sb("cqb8", [PROJ + 1, 1])

        cq = sb("cq", [PROJ + 1, 2, N])
        ck = sb("ck", [PROJ + 1, 2, N])
        cv = sb("cv", [P, 2, T, P])
        nmax = sb("nmax", [P, 2, T])
        rsum = sb("rsum", [P, 2, T])
        rinv = sb("rinv", [P, T])
        gsc = sb("gsc", [P, T])
        prob = sb("prob", [P, T, N])
        probT = sb("probT", [P, T, N])
        t1 = sb("t1", [P, 2, T, P])
        st1 = sb("st1", [P, T, 6])
        mv1 = sb("mv1", [P, T, 2])
        ve1 = sb("ve1", [P, T])
        rs1 = sb("rs1", [P, T])
        xn = sb("xn", [P, T, P])
        xnT = sb("xnT", [P, N])
        qT = sb("qT", [P, N])
        kT = sb("kT", [P, B, N])
        vt = sb("vt", [P, B, T * P])
        qk = sb("qk", [P, B, N])
        den = sb("den", [P, T * H])
        denm = sb("denm", [P, T * H])
        dinv = sb("dinv", [P, T * H])
        sco = sb("sco", [P, B, T * H])
        num = sb("num", [P, B, T * P])
        attT = sb("attT", [P, N])
        t2 = sb("t2", [P, NT, P])
        st2 = sb("st2", [P, T, 6])
        mv2 = sb("mv2", [P, T, 2])
        ve2 = sb("ve2", [P, T])
        rs2 = sb("rs2", [P, T])
        xrow = sb("xrow", [P, NT, TOP_K, ROW])
        x2T = sb("x2T", [P, N])
        top = sb("top", [P, T, 8])
        topi = sb("topi", [P, T, 8], U32)
        gap = sb("gap", [P, T])
        eg = sb("eg", [P, T])
        eg1 = sb("eg1", [P, T])
        wfirst = sb("wfirst", [P, T])
        chosen = sb("chosen", [P, T, TOP_K])
        mask = sb("mask", [P, T * TOP_K, E])
        hits = sb("hits", [P, T, E], BF16)
        seen = sb("seen", [P, NT + 1, E], BF16)
        base = sb("base", [P, T, E])
        where = sb("where", [P, T * TOP_K, E])
        slot = sb("slot", [P, NT * TOP_K], I32)
        cnt = sb("cnt", [1, E])
        up = sb("up", [1, E], I32)
        nbi = sb("nbi", [1, E], I32)
        nblk = sb("nblk", [1, E])
        one8 = sb("one8", [1, E])
        ends = sb("ends", [1, E])
        past = sb("past", [1, BLOCKS, E])
        skipped = sb("skipped", [1, BLOCKS, E])
        exp_f = sb("exp_f", [1, BLOCKS])
        first_f = sb("first_f", [1, BLOCKS])
        rel_f = sb("rel_f", [1, BLOCKS])
        relp_f = sb("relp_f", [1, BLOCKS])
        row_f = sb("row_f", [1, BLOCKS])
        table = sb("table", [1, T_END], I32)
        pad = sb("pad", [P, ROW])
        xb = sb("xb", [P, UNROLL, ROW])
        wd = sb("wd", [P, UNROLL, 2])
        xbT = sb("xbT", [P, UNROLL, P])
        gate = sb("gate", [P, UNROLL, F])
        hid = sb("hid", [P, UNROLL, F])
        hidT = sb("hidT", [P, UNROLL, FK, P])
        yb = sb("yb", [P, UNROLL, P])
        goes = sb("goes", [P, UNROLL], I32)
        y1 = sb("y1", [P, NT, P])
        y2 = sb("y2", [P, NT, P])

        ps = ctx.enter_context(nc.psum_tensor("ps", [P, 8, 512], F32))
        bank = lambda n: ps[:, n, :]
        ps_cqk = bank(0).rearrange("p (a n) -> p a n", a=2)
        ps_pT = bank(0).rearrange("p (k m) -> p k m", k=T)
        ps_sim = bank(1).rearrange("p (t n) -> p t n", t=T)
        ps_cv = bank(2)[:, 0:T * P].rearrange("p (t c) -> p t c", t=T)
        ps_co = bank(2)[:, T * P:2 * T * P].rearrange("p (t c) -> p t c", t=T)
        ps_xT = bank(3)[:, 0:N]
        ps_aT = bank(3)[:, N:2 * N]
        ps_qk = bank(4).rearrange("p (a n) -> p a n", a=2)
        ps_v = bank(5)[:, 0:T * P].rearrange("p (t c) -> p t c", t=T)
        ps_y = bank(5)[:, T * P:2 * T * P].rearrange("p (t c) -> p t c", t=T)
        ps_sc = bank(6)[:, 0:B * T * H].rearrange("p (j g) -> p j g", j=B)
        ps_x2T = bank(7)[:, 0:N]
        ps_log = bank(7)[:, N:N + T * E].rearrange("p (t e) -> p t e", t=T)
        ps_rank = bank(7)[:, N + T * E:N + 2 * T * E].rearrange("p (t e) -> p t e", t=T)
        ps_cnt = bank(7)[0:1, N + 2 * T * E:N + 2 * T * E + E]
        ps_xbT = bank(0)[:, 0:P]
        ps_hT = bank(1)[:, 0:FK * P].rearrange("p (k s) -> p k s", k=FK)
        ps_yb = bank(2)[:, 0:P]
        ps_gu = [bank(3 + n) for n in range(UNROLL)]

        ld_conv = sem("ld_conv")
        ld_x = [sem(f"ld_x{i}") for i in range(B)]
        ld_vec = sem("ld_vec")
        ld_bias = sem("ld_bias")
        ld_tri = sem("ld_tri")
        ld_dest = sem("ld_dest")
        ld_lin = sem("ld_lin")
        ld_cst = sem("ld_cst")
        ld_w13 = sem("ld_w13")
        bias_ready = sem("bias_ready")
        tri_ready = sem("tri_ready")
        cqb_ready = sem("cqb_ready")
        dest_ready = sem("dest_ready")
        pad_ready = sem("pad_ready")
        cqk_done = sem("cqk_done")
        cqk_read = sem("cqk_read")
        cv_done = sem("cv_done")
        cv_read = sem("cv_read")
        sim_done = sem("sim_done")
        max_done = sem("max_done")
        exp_done = sem("exp_done")
        pT_done = sem("pT_done")
        pT_read = sem("pT_read")
        co_done = sem("co_done")
        t1_done = sem("t1_done")
        ve1_done = sem("ve1_done")
        rs1_done = sem("rs1_done")
        xn_done = sem("xn_done")
        xT_done = sem("xT_done")
        xT_read = sem("xT_read")
        lqk_done = sem("lqk_done")
        lqk_read = sem("lqk_read")
        lv_done = sem("lv_done")
        lv_read = sem("lv_read")
        qk_done = sem("qk_done")
        sc_done = sem("sc_done")
        sco_done = sem("sco_done")
        att_done = sem("att_done")
        aT_done = sem("aT_done")
        aT_read = sem("aT_read")
        y_done = sem("y_done")
        t2_done = sem("t2_done")
        ve2_done = sem("ve2_done")
        rs2_done = sem("rs2_done")
        xrow_done = sem("xrow_done")
        x2T_done = sem("x2T_done")
        x2T_read = sem("x2T_read")
        log_done = sem("log_done")
        gap_done = sem("gap_done")
        eg_done = sem("eg_done")
        w_done = sem("w_done")
        hits_done = sem("hits_done")
        rank_done = sem("rank_done")
        slot_done = sem("slot_done")
        scattered = sem("scattered")
        cnt_done = sem("cnt_done")
        table_done = sem("table_done")
        pads_stored = sem("pads_stored")
        dve = sem("dve")
        xb_loaded = [sem(f"xb_loaded{n}") for n in range(UNROLL)]
        xbT_done = sem("xbT_done")
        xbT_read = sem("xbT_read")
        gu_done = sem("gu_done")
        gate_done = sem("gate_done")
        hid_done = sem("hid_done")
        hT_done = sem("hT_done")
        hT_read = sem("hT_read")
        yb_done_pe = sem("yb_done_pe")
        yb_done = sem("yb_done")
        goes_done = sem("goes_done")
        taken = sem("taken")
        store_turns = sem("store_turns")
        yb_stored = [sem(f"yb_stored{n}") for n in range(UNROLL)]
        y_loaded = [sem(f"y_loaded{n}") for n in range(4)]
        sum_done = sem("sum_done")
        out_stored = sem("out_stored")

        block = ctx.enter_context(nc.Block())
        rows_y_v = rows_y.rearrange("(c p t) d -> c p t d", c=TOP_K, p=P)

        @block.sync
        def _(sp):
            sp.dma_start(X[:, 0, :], x_ch[:, 0, :]).then_inc(ld_x[0], 16)
            sp.dma_start(WC[:, :], w_conv).then_inc(ld_conv, 16)
            sp.dma_start(VEC[:, :], vecs).then_inc(ld_vec, 16)
            sp.dma_start(CF[:, :], cst_f).then_inc(ld_cst, 16)
            sp.dma_start(XT[:, 0, :, :], x_tok[:, 0, :, :]).then_inc(ld_x[0], 16)
            sp.dma_start(BR[:, :], bias_rows).then_inc(ld_bias, 16)
            sp.dma_start(WL[:, :], w_lin).then_inc(ld_lin, 16)
            sp.dma_start(WR[:, :], w_router).then_inc(ld_lin, 16)
            sp.dma_start(TRI32[:, :], cst_tri).then_inc(ld_tri, 16)
            sp.dma_start(DEST[:, :], cst_dest).then_inc(ld_dest, 16)
            for i in range(1, B):
                sp.dma_start(X[:, i, :], x_ch[:, i, :]).then_inc(ld_x[i], 16)
                sp.dma_start(XT[:, i, :, :], x_tok[:, i, :, :]).then_inc(ld_x[i], 16)
            sp.dma_start(W13[:, :], w13).then_inc(ld_w13, 16)
            sp.dma_start(W2[:, :], w2).then_inc(ld_w13, 16)

            sp.wait_ge(pad_ready, 2)
            sp.dma_start(rows_x[DUMMY:DUMMY + P, :], pad[:, :]).then_inc(pads_stored, 16)
            sp.wait_ge(table_done, 1)
            for e in range(E):
                row = sp.value_load(table[0:1, T_PAD + e:T_PAD + e + 1], min_val=0, max_val=DUMMY - P)
                sp.dma_start(rows_x[bass.ds(row, P), :], pad[:, :]).then_inc(pads_stored, 16)
            sp.wait_ge(pads_stored, 16 * (E + 1))
            sp.wait_ge(scattered, 16 * NT * TOP_K)

            def load(s, n, used=None):
                row = sp.value_load(table[0:1, bass.ds(s, 1)], min_val=0, max_val=DUMMY)
                if used is not None:
                    sp.wait_ge(xbT_done, used)
                    sp.wait_ge(taken, used)
                sp.dma_start(xb[:, n, :], rows_x[bass.ds(row, P), :]).then_inc(xb_loaded[n], 16)

            for n in range(UNROLL):
                load(n, n)
            with sp.Fori(1, TURNS) as turn:
                for n in range(UNROLL):
                    s = turn * UNROLL + n
                    load(s, n, s - UNROLL + 1)

            for n in range(UNROLL):
                sp.wait_ge(yb_stored[n], 16 * TURNS)
            for q in range(PARTS):
                a, b = q * NT // PARTS, (q + 1) * NT // PARTS
                sp.dma_start(y1[:, a:b, :], rows_y_v[0, :, a:b, :]).then_inc(y_loaded[q], 16)
                sp.dma_start(y2[:, a:b, :], rows_y_v[1, :, a:b, :]).then_inc(y_loaded[q], 16)
            for q in range(PARTS):
                a, b = q * NT // PARTS, (q + 1) * NT // PARTS
                sp.wait_ge(sum_done, q + 1)
                sp.dma_start(out[:, a:b, :], y2[:, a:b, :]).then_inc(out_stored, 16)
            sp.wait_ge(out_stored, 16 * PARTS)

        @block.gpsimd
        def _(pool):
            pool.memset(pad[:, 0:DEST_COL], 0.0).then_inc(pad_ready, 1)
            pool.memset(pad[:, DEST_COL:ROW], float(SKIP)).then_inc(pad_ready, 1)
            pool.wait_ge(ld_dest, 16)
            pool.tensor_copy(xrow[:, :, :, DEST_COL].rearrange("p t c -> p (t c)"),
                             DEST[:, :]).then_inc(dest_ready, 1)

            def rstd_lin(i):
                pool.wait_ge(ve1_done, i + 1)
                if i >= 1:
                    pool.wait_ge(xn_done, 2 * i)
                pool.tensor_tensor(rs1[:, :], ve1[:, :], CF[:, C_HALF:C_HALF + T], ALU.pow).then_inc(rs1_done, 1)

            def rstd_ffn(i):
                pool.wait_ge(ve2_done, i + 1)
                if i >= 1:
                    pool.wait_ge(xrow_done, 2 * i)
                pool.tensor_tensor(rs2[:, :], ve2[:, :], CF[:, C_HALF:C_HALF + T], ALU.pow).then_inc(rs2_done, 1)

            def products(i):
                pool.wait_ge(lqk_read, 2 * (i + 1))
                if i >= 1:
                    pool.wait_ge(sc_done, i)
                pool.tensor_tensor(qk[:, 0:i + 1, :], kT[:, 0:i + 1, :],
                                   qT[:, :].unsqueeze(1).broadcast_to([P, i + 1, N]), ALU.mult).then_inc(qk_done, 1)

            def scatter(i):
                pool.wait_ge(slot_done, i + 1)
                pool.wait_ge(w_done, 2 * (i + 1))
                pool.wait_ge(xrow_done, 2 * (i + 1))
                pool.wait_ge(dest_ready, 1)
                for t in range(T * i, T * i + T):
                    for c in range(TOP_K):
                        g = t * TOP_K + c
                        pool.indirect_dma_start(rows_x, bass.IndirectOffsetOnAxis(ap=slot[:, g:g + 1], axis=0),
                                                xrow[:, t, c, :], None, bounds_check=DUMMY + P - 1,
                                                oob_is_err=False).then_inc(scattered, 16)

            for step in range(B + 2):
                i, j, k = step, step - 1, step - 2
                if 0 <= j < B:
                    products(j)
                if 0 <= k < B:
                    scatter(k)
                if i < B:
                    rstd_lin(i)
                if 0 <= j < B:
                    rstd_ffn(j)

            last_row = pool.to_reg(TOP_K * TOKENS - 1)

            def store(n, count):
                pool.wait_ge(goes_done, count)
                pool.wait_ge(yb_done, count)
                pool.sem_inc(store_turns, 1)
                pool.indirect_dma_start(
                    rows_y, bass.IndirectOffsetOnAxis(ap=goes[:, n:n + 1], axis=0),
                    yb[:, n, :], None, bounds_check=last_row,
                    oob_is_err=False).then_inc(yb_stored[n], 16)

            with pool.Fori(0, TURNS) as turn:
                for n in range(UNROLL):
                    store(n, turn * UNROLL + n + 1)

        @block.scalar
        def _(act):
            act.wait_ge(ld_vec, 16)
            act.mul(cqb8[:, :], VEC[0:PROJ + 1, V_CQB:V_CQB + 1], PROJ ** -0.5).then_inc(cqb_ready, 1)

            def conv_qk(i):
                b = i % 2
                act.wait_ge(cqk_done, i + 1)
                if i == 0:
                    act.wait_ge(cqb_ready, 1)
                if i >= 2:
                    act.wait_ge(sim_done, i - 1)
                    act.wait_ge(co_done, i - 1)
                act.activation(cq[:, b, :], ps_cqk[0:PROJ + 1, 0, :], ACT.Identity, bias=cqb8[:, :],
                               scale=PROJ ** -0.5).then_inc(cqk_read, 1)
                act.activation(ck[:, b, :], ps_cqk[0:PROJ + 1, 1, :], ACT.Identity,
                               bias=VEC[0:PROJ + 1, V_CKB:V_CKB + 1]).then_inc(cqk_read, 1)
                act.wait_ge(cv_done, i + 1)
                act.activation(cv[:, b, :, :], ps_cv, ACT.Copy).then_inc(cv_read, 1)

            def conv_exp(i):
                b = i % 2
                act.wait_ge(max_done, i + 1)
                if i >= 1:
                    act.wait_ge(pT_done, i)
                for t in range(T):
                    act.activation(prob[:, t, :], ps_sim[:, t, :], ACT.Exp, bias=nmax[:, b, t:t + 1],
                                   accum_out=rsum[:, b, t:t + 1]).then_inc(exp_done, 1)

            def conv_pT(i):
                act.wait_ge(pT_done, i + 1)
                if i >= 1:
                    act.wait_ge(co_done, i)
                act.activation(probT[:, :, :], ps_pT, ACT.Copy).then_inc(pT_read, 1)

            def lin_xT(i):
                act.wait_ge(xT_done, i + 1)
                if i >= 1:
                    act.wait_ge(lv_done, i)
                act.activation(xnT[:, :], ps_xT, ACT.Copy).then_inc(xT_read, 1)

            def lin_qkv(i):
                act.wait_ge(lqk_done, i + 1)
                if i >= 1:
                    act.wait_ge(qk_done, i)
                act.activation(qT[:, :], ps_qk[:, 0, :], ACT.Relu, bias=VEC[:, V_QB:V_QB + 1]).then_inc(lqk_read, 1)
                act.activation(kT[:, i, :], ps_qk[:, 1, :], ACT.Relu, bias=VEC[:, V_KB:V_KB + 1]).then_inc(lqk_read, 1)
                act.wait_ge(lv_done, i + 1)
                act.activation(vt[:, i, :].rearrange("p (t c) -> p t c", t=T), ps_v, ACT.Copy).then_inc(lv_read, 1)

            def lin_aT(i):
                act.wait_ge(aT_done, i + 1)
                if i >= 1:
                    act.wait_ge(y_done, i)
                act.activation(attT[:, :], ps_aT, ACT.Copy).then_inc(aT_read, 1)

            def route_xT(i):
                act.wait_ge(x2T_done, i + 1)
                if i >= 1:
                    act.wait_ge(log_done, i)
                act.activation(x2T[:, :], ps_x2T, ACT.Copy).then_inc(x2T_read, 1)

            def route_exp(i):
                act.wait_ge(gap_done, i + 1)
                if i >= 1:
                    act.wait_ge(w_done, 2 * i)
                act.activation(eg[:, :], gap[:, :], ACT.Exp).then_inc(eg_done, 1)

            for step in range(B + 2):
                i, j, k = step, step - 1, step - 2
                if i < B:
                    conv_qk(i)
                if 0 <= j < B:
                    lin_xT(j)
                if i < B:
                    conv_exp(i)
                if 0 <= j < B:
                    lin_qkv(j)
                if 0 <= k < B:
                    route_xT(k)
                if i < B:
                    conv_pT(i)
                if 0 <= k < B:
                    route_exp(k)
                if 0 <= j < B:
                    lin_aT(j)

            def turn_x(s, n, count):
                act.wait_ge(xbT_done, count)
                act.activation(xbT[:, n, :], ps_xbT, ACT.Copy).then_inc(xbT_read, 1)

            def silu(s, n, count):
                act.wait_ge(gu_done, count)
                act.activation(gate[:, n, :], ps_gu[n][:, 0:F], ACT.Silu).then_inc(gate_done, 1)

            turn_x(0, 0, 1)
            turn_x(1, 1, 2)
            silu(0, 0, 1)
            turn_x(2, 2, 3)
            silu(1, 1, 2)

            def step_of(s, n, base):
                m = (n + 2) % UNROLL
                act.wait_ge(gu_done, base + n)
                turn_x(s + 2, m, base + n + 3)
                act.wait_ge(hid_done, base + n - 1)
                silu(s + 1, (n + 1) % UNROLL, base + n + 2)

            for n in (1, 2):
                act.wait_ge(gu_done, n)
                turn_x(n + 2, (n + 2) % UNROLL, n + 3)
                if n >= 2:
                    act.wait_ge(hid_done, n - 1)
                silu(n + 1, (n + 1) % UNROLL, n + 2)
            with act.Fori(1, TURNS - 1) as turn:
                for n in range(UNROLL):
                    step_of(turn * UNROLL + n, n, turn * UNROLL)
            last = (TURNS - 1) * UNROLL
            step_of(last, 0, last)
            act.wait_ge(hid_done, last)
            silu(last + 2, 2, last + 3)

        @block.tensor
        def _(pe):
            def conv_proj(i):
                if i == 0:
                    pe.wait_ge(ld_conv, 16)
                pe.wait_ge(ld_x[i], 32)
                if i >= 1:
                    pe.wait_ge(pT_read, i)
                pe.matmul(ps_cqk[0:PROJ + 1, 0, :], wq, X[:, i, :], start=True, stop=True)
                pe.matmul(ps_cqk[0:PROJ + 1, 1, :], wk, X[:, i, :], start=True, stop=True).then_inc(cqk_done, 1)
                if i >= 1:
                    pe.wait_ge(t1_done, 2 * i)
                for t in range(T):
                    last = pe.matmul(ps_cv[:, t, :], X[:, i, t * P:(t + 1) * P], wv, start=True, stop=True)
                last.then_inc(cv_done, 1)

            def conv_scores(i):
                b = i % 2
                pe.wait_ge(cqk_read, 2 * (i + 1))
                if i >= 1:
                    pe.wait_ge(exp_done, 2 * i)
                for t in range(T):
                    last = pe.matmul(ps_sim[:, t, :], cq[:, b, t * P:(t + 1) * P], ck[:, b, :], start=True, stop=True)
                last.then_inc(sim_done, 1)

            def conv_turn(i):
                if i == 0:
                    pe.wait_ge(ld_cst, 16)
                pe.wait_ge(exp_done, 2 * (i + 1))
                for k in range(T):
                    for t in range(T):
                        last = pe.transpose(ps_pT[:, k, t * P:(t + 1) * P], prob[:, t, k * P:(k + 1) * P], ident)
                last.then_inc(pT_done, 1)

            def conv_out(i):
                b = i % 2
                pe.wait_ge(pT_read, i + 1)
                pe.wait_ge(cv_read, i + 1)
                for t in range(T):
                    for k in range(T):
                        last = pe.matmul(ps_co[:, t, :], probT[:, k, t * P:(t + 1) * P], cv[:, b, k, :],
                                         start=(k == 0), stop=(k == T - 1))
                last.then_inc(co_done, 1)

            def lin_turn(i):
                pe.wait_ge(xn_done, 2 * (i + 1))
                if i >= 1:
                    pe.wait_ge(aT_read, i)
                for t in range(T):
                    last = pe.transpose(ps_xT[:, t * P:(t + 1) * P], xn[:, t, :], ident)
                last.then_inc(xT_done, 1)

            def lin_proj(i):
                if i == 0:
                    pe.wait_ge(ld_lin, 32)
                    pe.wait_ge(bias_ready, 1)
                pe.wait_ge(xT_read, i + 1)
                if i >= 1:
                    pe.wait_ge(lqk_read, 2 * i)
                pe.matmul(ps_qk[:, 0, :], lq, xnT[:, :], start=True, stop=True)
                pe.matmul(ps_qk[:, 1, :], lk, xnT[:, :], start=True, stop=True).then_inc(lqk_done, 1)
                if i >= 1:
                    pe.wait_ge(t2_done, i)
                for t in range(T):
                    pe.matmul(ps_v[:, t, :], xnT[:, t * P:(t + 1) * P], lv, start=True, stop=False)
                    last = pe.matmul(ps_v[:, t, :], ONES[:, :], vb_row, start=False, stop=True)
                last.then_inc(lv_done, 1)

            def lin_scores(i):
                pe.wait_ge(qk_done, i + 1)
                if i >= 1:
                    pe.wait_ge(sco_done, i)
                for j in range(i + 1):
                    heads = CF[:, C_COS + (i - j) * H:C_COS + (i - j + 1) * H]
                    for t in range(T):
                        last = pe.matmul(ps_sc[:, j, t * H:(t + 1) * H], qk[:, j, t * P:(t + 1) * P], heads,
                                         start=True, stop=True)
                last.then_inc(sc_done, 1)

            def lin_out_turn(i):
                pe.wait_ge(att_done, i + 1)
                for t in range(T):
                    last = pe.transpose(ps_aT[:, t * P:(t + 1) * P], num[:, 0, t * P:(t + 1) * P], ident)
                last.then_inc(aT_done, 1)

            def lin_out(i):
                pe.wait_ge(aT_read, i + 1)
                pe.wait_ge(lv_read, i + 1)
                for t in range(T):
                    pe.matmul(ps_y[:, t, :], attT[:, t * P:(t + 1) * P], lo, start=True, stop=False)
                    last = pe.matmul(ps_y[:, t, :], ONES[:, :], ob_row, start=False, stop=True)
                last.then_inc(y_done, 1)

            def route_turn(i):
                pe.wait_ge(xrow_done, 2 * (i + 1))
                if i >= 1:
                    pe.wait_ge(slot_done, i)
                for t in range(T):
                    last = pe.transpose(ps_x2T[:, t * P:(t + 1) * P], xrow[:, i * T + t, 0, 0:P], ident)
                last.then_inc(x2T_done, 1)

            def route_logits(i):
                pe.wait_ge(x2T_read, i + 1)
                for t in range(T):
                    last = pe.matmul(ps_log[:, t, :], x2T[:, t * P:(t + 1) * P], WR[:, :], start=True, stop=True)
                last.then_inc(log_done, 1)

            def route_rank(i):
                pe.wait_ge(hits_done, 3 * (i + 1))
                pe.wait_ge(tri_ready, 1)
                for t in range(T):
                    pe.matmul(ps_rank[:, t, :], TRI[:, 0:P], hits[:, t, :], start=True, stop=False)
                    last = pe.matmul(ps_rank[:, t, :], TRI[:, P:2 * P], seen[:, i * T + t, :], start=False, stop=True)
                last.then_inc(rank_done, 1)

            for step in range(B + 2):
                i, j, k = step, step - 1, step - 2
                if i < B:
                    conv_proj(i)
                if 0 <= j < B:
                    lin_turn(j)
                if i < B:
                    conv_scores(i)
                if 0 <= j < B:
                    lin_proj(j)
                if 0 <= k < B:
                    route_turn(k)
                    route_logits(k)
                if i < B:
                    conv_turn(i)
                if 0 <= j < B:
                    lin_scores(j)
                if 0 <= k < B:
                    route_rank(k)
                if i < B:
                    conv_out(i)
                if 0 <= j < B:
                    lin_out_turn(j)
                    lin_out(j)

            pe.wait_ge(slot_done, B)
            pe.matmul(ps_cnt, TRI[:, P:P + 1], seen[:, NT, :], start=True, stop=True).then_inc(cnt_done, 1)

            def turn_x(s, n, count, before):
                if before is not None:
                    pe.wait_ge(xbT_read, before)
                pe.wait_ge(xb_loaded[n], count)
                pe.transpose(ps_xbT, xb[:, n, 0:P], ident).then_inc(xbT_done, 1)

            def expert(s):
                return pe.value_load(table[0:1, bass.ds(T_EXPERT + s, 1)], min_val=0, max_val=E - 1)

            def gate_up(s, n, count, before):
                e = expert(s)
                if before is not None:
                    pe.wait_ge(hid_done, before)
                pe.wait_ge(xbT_read, count)
                pe.matmul(ps_gu[n], xbT[:, n, :], W13[:, bass.ds(e * (2 * F), 2 * F)], start=True, stop=True)\
                  .then_inc(gu_done, 1)

            def turn_h(s, n, count, before):
                if before is not None:
                    pe.wait_ge(hT_read, before)
                pe.wait_ge(hid_done, count)
                for k in range(FK):
                    last = pe.transpose(ps_hT[:, k, :], hid[:, n, k * P:(k + 1) * P], ident)
                last.then_inc(hT_done, 1)

            def down(s, n, count, before):
                e = expert(s)
                if before is not None:
                    pe.wait_ge(yb_done, before)
                pe.wait_ge(hT_read, count)
                for k in range(FK):
                    last = pe.matmul(ps_yb, hidT[:, n, k, :], W2[:, bass.ds(e * (FK * P) + k * P, P)],
                                     start=(k == 0), stop=(k == FK - 1))
                last.then_inc(yb_done_pe, 1)

            pe.wait_ge(ld_w13, 32)
            pe.wait_ge(table_done, 1)
            turn_x(0, 0, 16, None)
            turn_x(1, 1, 16, 1)
            gate_up(0, 0, 1, None)

            def step_of(s, n, turn, first=False, last=False):
                if not (last and n >= 1):
                    turn_x(s + 2, (n + 2) % UNROLL, (turn + (1 if n == 0 else 2)) * 16, s + 2)
                if not (last and n == 2):
                    gate_up(s + 1, (n + 1) % UNROLL, s + 2, None if first and n < 2 else s - 1)
                turn_h(s, n, s + 1, None if first and n == 0 else s)
                if not (first and n == 0):
                    down(s - 1, (n + 2) % UNROLL, s, None if first and n == 1 else s - 1)

            for n in range(UNROLL):
                step_of(n, n, 0, first=True)
            with pe.Fori(1, TURNS - 1) as turn:
                for n in range(UNROLL):
                    step_of(turn * UNROLL + n, n, turn)
            for n in range(UNROLL):
                step_of((TURNS - 1) * UNROLL + n, n, TURNS - 1, last=True)
            down(BLOCKS - 1, UNROLL - 1, BLOCKS, BLOCKS - 1)

        @block.vector
        def _(dv):
            links = [0]

            def link(ins):
                links[0] += 1
                ins.then_inc(dve, 1)
                dv.wait_ge(dve, links[0])

            dv.memset(ONES[:, :], 1.0)
            link(dv.memset(BIAS[:, :], 0.0))
            dv.memset(seen[:, 0, :], 0.0)
            dv.memset(one8[:, :], 1.0)
            dv.wait_ge(ld_bias, 16)
            link(dv.tensor_copy(b_part[0][:, :], BR[:, :]))
            link(dv.tensor_tensor(b_rest[0][:, :], BR[:, :], b_part[0][:, :], ALU.subtract))
            link(dv.tensor_copy(b_part[1][:, :], b_rest[0][:, :]))
            link(dv.tensor_tensor(b_rest[1][:, :], b_rest[0][:, :], b_part[1][:, :], ALU.subtract))
            link(dv.tensor_copy(b_part[2][:, :], b_rest[1][:, :]))
            for n in range(3):
                last = dv.tensor_copy(BIAS[32 * n:32 * n + 1, :], b_part[n][32 * n:32 * n + 1, :])
                if n < 2:
                    link(last)
            last.then_inc(bias_ready, 1)
            dv.wait_ge(ld_tri, 16)
            dv.tensor_copy(TRI[:, :], TRI32[:, :]).then_inc(tri_ready, 1)
            dv.wait_ge(ld_vec, 16)
            dv.wait_ge(ld_cst, 16)

            def conv_max(i):
                dv.wait_ge(sim_done, i + 1)
                if i >= 2:
                    dv.wait_ge(exp_done, 2 * (i - 1))
                dv.tensor_reduce(nmax[:, i % 2, :], ps_sim, AX.X, ALU.max, negate=True).then_inc(max_done, 1)

            def conv_add(i):
                b = i % 2
                dv.wait_ge(exp_done, 2 * (i + 1))
                link(dv.reciprocal(rinv[:, :], rsum[:, b, :]))
                link(dv.tensor_scalar(gsc[:, :], rinv[:, :], VEC[:, V_GAMMA:V_GAMMA + 1], None, ALU.mult))
                dv.wait_ge(co_done, i + 1)
                dv.wait_ge(ld_x[i], 32)
                if i >= 2:
                    dv.wait_ge(t2_done, i - 1)
                for t in range(T):
                    last = dv.scalar_tensor_tensor(out=t1[:, b, t, :], in0=ps_co[:, t, :], scalar=gsc[:, t:t + 1],
                                                   in1=XT[:, i, t, :], op0=ALU.mult, op1=ALU.add)
                    last.then_inc(t1_done, 1)
                dv.wait_ge(t1_done, 2 * (i + 1))
                if i >= 1:
                    dv.wait_ge(rs1_done, i)
                norm_stats(t1[:, b, :, :], st1, mv1, ve1, ve1_done)

            def norm_stats(x, st, mv, ve, done):
                for t in range(T):
                    last = dv.bn_stats(st[:, t, :], x[:, t, :])
                link(last)
                for t in range(T):
                    last = dv.bn_aggr(mv[:, t, :], st[:, t, :])
                link(last)
                dv.tensor_scalar(ve[:, :], mv[:, :, 1], LN_EPS, None, ALU.add).then_inc(done, 1)

            def lin_norm(i):
                dv.wait_ge(rs1_done, i + 1)
                if i >= 1:
                    dv.wait_ge(xT_done, i)
                for t in range(T):
                    dv.tensor_scalar(xn[:, t, :], t1[:, i % 2, t, :], mv1[:, t, 0:1], rs1[:, t:t + 1],
                                     ALU.subtract, ALU.mult).then_inc(xn_done, 1)

            def lin_weights(i):
                dv.wait_ge(sc_done, i + 1)
                sc = ps_sc[:, 0:i + 1, :]
                link(dv.tensor_reduce(den[:, :], sc.rearrange("p j g -> p g j"), AX.X, ALU.add))
                link(dv.tensor_scalar(denm[:, :], den[:, :], DEN_EPS, None, ALU.max))
                link(dv.reciprocal(dinv[:, :], denm[:, :]))
                dv.tensor_tensor(sco[:, 0:i + 1, :], sc, dinv[:, :].unsqueeze(1).broadcast_to([P, i + 1, T * H]),
                                 ALU.mult).then_inc(sco_done, 1)

            def lin_values(i):
                dv.wait_ge(sco_done, i + 1)
                dv.wait_ge(lv_read, i + 1)
                if i >= 1:
                    dv.wait_ge(aT_done, i)
                m = i + 1
                w = sco[:, 0:m, :].rearrange("p j g -> p (j g)").unsqueeze(2).broadcast_to([P, m * T * H, D])
                ins = dv.tensor_tensor(num[:, 0:m, :].rearrange("p j (g d) -> p (j g) d", d=D),
                                       vt[:, 0:m, :].rearrange("p j (g d) -> p (j g) d", d=D), w, ALU.mult)
                while m > 1:
                    half = m // 2
                    link(ins)
                    ins = dv.tensor_tensor(num[:, 0:half, :], num[:, 0:half, :], num[:, m - half:m, :], ALU.add)
                    m -= half
                ins.then_inc(att_done, 1)

            def lin_add(i):
                dv.wait_ge(y_done, i + 1)
                x = t2[:, i * T:(i + 1) * T, :]
                dv.tensor_tensor(x, ps_y, t1[:, i % 2, :, :], ALU.add).then_inc(t2_done, 1)
                dv.wait_ge(t2_done, i + 1)
                if i >= 1:
                    dv.wait_ge(rs2_done, i)
                norm_stats(x, st2, mv2, ve2, ve2_done)

            def route_norm(i):
                dv.wait_ge(rs2_done, i + 1)
                for t in range(T):
                    dv.tensor_scalar(xrow[:, i * T + t, :, 0:P],
                                     t2[:, i * T + t, :].unsqueeze(1).broadcast_to([P, TOP_K, P]),
                                     mv2[:, t, 0:1], rs2[:, t:t + 1], ALU.subtract, ALU.mult).then_inc(xrow_done, 1)

            def route_top(i):
                dv.wait_ge(log_done, i + 1)
                for t in range(T):
                    last = dv.max(top[:, t, :], ps_log[:, t, :])
                link(last)
                for t in range(T):
                    last = dv.max_index(topi[:, t, :], top[:, t, :], ps_log[:, t, :])
                if i >= 1:
                    dv.wait_ge(eg_done, i)
                dv.tensor_tensor(gap[:, :], top[:, :, 1], top[:, :, 0], ALU.subtract).then_inc(gap_done, 1)
                link(last)
                link(dv.tensor_copy(chosen[:, :, :], topi[:, :, 0:TOP_K]))
                g = T * TOP_K
                link(dv.tensor_tensor(mask[:, :, :],
                                      CF[:, C_EXPERT:C_EXPERT + E].unsqueeze(1).broadcast_to([P, g, E]),
                                      chosen[:, :, :].rearrange("p t c -> p (t c)").unsqueeze(2).broadcast_to([P, g, E]),
                                      ALU.is_equal))
                m = mask[:, :, :].rearrange("p (t c) e -> p t c e", c=TOP_K)
                if i >= 1:
                    dv.wait_ge(rank_done, i)
                dv.tensor_tensor(hits[:, :, :], m[:, :, 0, :], m[:, :, 1, :], ALU.add).then_inc(hits_done, 1)
                dv.wait_ge(hits_done, 3 * i + 1)
                for t in range(T):
                    n = i * T + t
                    dv.tensor_tensor(seen[:, n + 1, :], seen[:, n, :], hits[:, t, :], ALU.add).then_inc(hits_done, 1)
                    dv.wait_ge(hits_done, 3 * i + 2 + t)

            def route_weights(i):
                dv.wait_ge(eg_done, i + 1)
                link(dv.tensor_scalar(eg1[:, :], eg[:, :], 1.0, None, ALU.add))
                link(dv.reciprocal(wfirst[:, :], eg1[:, :]))
                tiles = xrow[:, i * T:(i + 1) * T, :, :]
                dv.tensor_copy(tiles[:, :, 0, W_COL], wfirst[:, :]).then_inc(w_done, 1)
                dv.tensor_tensor(tiles[:, :, 1, W_COL], eg[:, :], wfirst[:, :], ALU.mult).then_inc(w_done, 1)

            def route_slots(i):
                dv.wait_ge(rank_done, i + 1)
                link(dv.tensor_tensor(base[:, :, :], ps_rank,
                                      CF[:, C_ECAP:C_ECAP + E].unsqueeze(1).broadcast_to([P, T, E]), ALU.add))
                link(dv.tensor_tensor(where[:, :, :].rearrange("p (t c) e -> p t c e", c=TOP_K),
                                      mask[:, :, :].rearrange("p (t c) e -> p t c e", c=TOP_K),
                                      base[:, :, :].unsqueeze(2).broadcast_to([P, T, TOP_K, E]), ALU.mult))
                g = T * TOP_K
                with nc.allow_low_precision(reason="whole numbers below 2 ** 24, summed in float32"):
                    dv.tensor_reduce(slot[:, i * g:(i + 1) * g], where[:, :, :], AX.X, ALU.add).then_inc(slot_done, 1)

            for step in range(B + 2):
                i, j, k = step, step - 1, step - 2
                if 0 <= j < B:
                    lin_norm(j)
                if 0 <= k < B:
                    route_norm(k)
                if i < B:
                    conv_max(i)
                if 0 <= k < B:
                    route_top(k)
                if 0 <= j < B:
                    lin_weights(j)
                if 0 <= k < B:
                    route_weights(k)
                    route_slots(k)
                if 0 <= j < B:
                    lin_values(j)
                if i < B:
                    conv_add(i)
                if 0 <= j < B:
                    lin_add(j)

            dv.wait_ge(cnt_done, 1)
            link(dv.tensor_copy(cnt[:, :], ps_cnt))
            link(dv.tensor_scalar(up[:, :], cnt[:, :], float(P - 1), None, ALU.add))
            link(dv.tensor_scalar(nbi[:, :], up[:, :], P.bit_length() - 1, None, ALU.logical_shift_right))
            link(dv.tensor_copy(nblk[:, :], nbi[:, :]))
            link(dv.tensor_tensor_scan(ends[:, :], one8[:, :], nblk[:, :], 0.0, ALU.mult, ALU.add))
            turn_of = CF[0:1, C_BLOCK:C_BLOCK + BLOCKS]
            link(dv.tensor_tensor(past[:, :, :], turn_of.unsqueeze(2).broadcast_to([1, BLOCKS, E]),
                                  ends[:, :].unsqueeze(1).broadcast_to([1, BLOCKS, E]), ALU.is_ge))
            link(dv.tensor_tensor(skipped[:, :, :], past[:, :, :],
                                  nblk[:, :].unsqueeze(1).broadcast_to([1, BLOCKS, E]), ALU.mult))
            link(dv.tensor_reduce(exp_f[:, :], past[:, :, :], AX.X, ALU.add))
            link(dv.tensor_reduce(first_f[:, :], skipped[:, :, :], AX.X, ALU.add))
            link(dv.tensor_tensor(rel_f[:, :], turn_of, first_f[:, :], ALU.subtract))
            link(dv.tensor_scalar(relp_f[:, :], rel_f[:, :], float(P), None, ALU.mult))
            link(dv.scalar_tensor_tensor(out=row_f[:, :], in0=exp_f[:, :], scalar=float(CAP), in1=relp_f[:, :],
                                         op0=ALU.mult, op1=ALU.add))
            dv.tensor_tensor(table[:, T_PAD:T_PAD + E], cnt[:, :], CF[0:1, C_ECAP:C_ECAP + E], ALU.add)
            dv.tensor_scalar(table[:, T_EXPERT:T_EXPERT + BLOCKS], exp_f[:, :], float(E - 1), None, ALU.min)
            dv.tensor_scalar(table[:, T_ROW:T_ROW + BLOCKS], row_f[:, :], float(DUMMY), None, ALU.min)\
              .then_inc(table_done, 1)

            def hidden(n, count):
                dv.wait_ge(gate_done, count)
                dv.tensor_tensor(hid[:, n, :], gate[:, n, :], ps_gu[n][:, F:2 * F], ALU.mult).then_inc(hid_done, 1)

            def hidden_T(n, count):
                dv.wait_ge(hT_done, count)
                dv.tensor_copy(hidT[:, n, :, :], ps_hT).then_inc(hT_read, 1)

            def weigh(n, count, stored):
                dv.wait_ge(yb_done_pe, count)
                if stored is not None:
                    dv.wait_ge(yb_stored[n], stored)
                dv.wait_ge(taken, count)
                dv.tensor_copy(goes[:, n:n + 1], wd[:, n, 1:2]).then_inc(goes_done, 1)
                dv.tensor_scalar(yb[:, n, :], ps_yb, wd[:, n, 0:1], None, ALU.mult).then_inc(yb_done, 1)

            def take(n, count, weighed=None):
                if weighed is not None:
                    dv.wait_ge(goes_done, weighed)
                    dv.wait_ge(yb_done, weighed)
                dv.wait_ge(xb_loaded[n], count)
                dv.tensor_copy(wd[:, n, :], xb[:, n, W_COL:ROW]).then_inc(taken, 1)

            def step_of(s, n, turn, first=False, last=False):
                hidden(n, s + 1)
                hidden_T(n, s + 1)
                if not (first and n == 0):
                    stored = (turn if n >= 1 else turn - 1) * 16
                    weigh((n + 2) % UNROLL, s, None if first else stored)
                if not (last and n >= 1):
                    take((n + 2) % UNROLL, (turn + (1 if n == 0 else 2)) * 16, None if first and n == 0 else s)

            take(0, 16)
            take(1, 16)
            for n in range(UNROLL):
                step_of(n, n, 0, first=True)
            with dv.Fori(1, TURNS - 1) as turn:
                for n in range(UNROLL):
                    step_of(turn * UNROLL + n, n, turn)
            for n in range(UNROLL):
                step_of((TURNS - 1) * UNROLL + n, n, TURNS - 1, last=True)
            weigh(UNROLL - 1, BLOCKS, (TURNS - 1) * 16)

            for q in range(PARTS):
                a, b = q * NT // PARTS, (q + 1) * NT // PARTS
                dv.wait_ge(y_loaded[q], 32)
                link(dv.tensor_tensor(y1[:, a:b, :], y1[:, a:b, :], t2[:, a:b, :], ALU.add))
                dv.tensor_tensor(y2[:, a:b, :], y1[:, a:b, :], y2[:, a:b, :], ALU.add).then_inc(sum_done, 1)


def kernel(x, L0_conv_wq, L0_conv_bq, L0_conv_wk, L0_conv_bk, L0_conv_wv, L0_conv_wkm, L0_conv_bkm, L0_conv_gamma,
           L1_attn_q_w, L1_attn_q_b, L1_attn_k_w, L1_attn_k_b, L1_attn_v_w, L1_attn_v_b, L1_attn_out_w,
           L1_attn_out_b, L1_ffn_router_w, L1_ffn_w1, L1_ffn_w2, L1_ffn_w3):
    import concourse.bacc as bacc
    from concourse.bass_utils import run_bass_kernel_spmd

    x3 = np.asarray(x).reshape(B, P, N)
    zero_col = np.zeros((P, 1), np.float32)
    vecs = np.zeros((P, V_END), np.float32)
    vecs[:, V_QB], vecs[:, V_KB] = L1_attn_q_b, L1_attn_k_b
    vecs[0:PROJ, V_CQB], vecs[PROJ, V_CQB] = L0_conv_bq, PROJ ** 0.5
    vecs[0:PROJ, V_CKB], vecs[PROJ, V_CKB] = L0_conv_bk, L0_conv_bkm[0]
    vecs[:, V_GAMMA] = L0_conv_gamma[0]
    bias_rows = np.zeros((65, 2 * P), np.float32)
    bias_rows[::32] = np.concatenate([L1_attn_v_b, L1_attn_out_b])
    cst_f, cst_tri, cst_dest = constants()
    w13 = np.concatenate([L1_ffn_w1, L1_ffn_w3], axis=2)
    arrays = {
        "x_ch": x3.transpose(1, 0, 2),
        "x_tok": x3.reshape(B, P, T, P).transpose(3, 0, 2, 1),
        "w_conv": np.concatenate([np.asarray(L0_conv_wq).T, zero_col, np.asarray(L0_conv_wk).T,
                                  np.asarray(L0_conv_wkm).T, np.asarray(L0_conv_wv).T], axis=1),
        "w_lin": np.concatenate([np.asarray(w).T for w in (L1_attn_q_w, L1_attn_k_w, L1_attn_v_w, L1_attn_out_w)],
                                axis=1),
        "w_router": np.asarray(L1_ffn_router_w),
        "w13": w13.transpose(1, 0, 2).reshape(P, E * 2 * F),
        "w2": np.asarray(L1_ffn_w2).reshape(E, FK, P, P).transpose(2, 0, 1, 3).reshape(P, E * FK * P),
        "vecs": vecs,
        "bias_rows": bias_rows,
        "cst_f": cst_f,
        "cst_tri": cst_tri,
        "cst_dest": cst_dest,
    }
    arrays = {f"in_{n}": np.ascontiguousarray(a) for n, a in arrays.items()}
    nc = bacc.Bacc("TRN2", target_bir_lowering=False, num_devices=1)
    args = [nc.dram_tensor(n, a.shape, mybir.dt.from_np(a.dtype), kind="ExternalInput").ap()
            for n, a in arrays.items()]
    args.append(nc.dram_tensor("out_tok", (P, NT, P), F32, kind="ExternalOutput").ap())
    hybrid_block(nc, *args)
    r = run_bass_kernel_spmd(nc, [arrays], core_ids=[0])
    got = r.results[0]["out_tok"]
    return got.reshape(P, B, T, P).transpose(1, 3, 2, 0).reshape(B, P, 16, 16)
```

```python
from contextlib import ExitStack

import numpy as np

import concourse.bass as bass
from concourse import mybir

ALU = mybir.AluOpType
ACT = mybir.ActivationFunctionType
AX = mybir.AxisListType
F32 = mybir.dt.float32
BF16 = mybir.dt.bfloat16
I32 = mybir.dt.int32
U32 = mybir.dt.uint32

P = 128
B = 8
N = 256
T = N // P
NT = B * T
TOKENS = B * N
PROJ = 64
H = 8
D = P // H
E = 8
F = 256
FK = F // P
TOP_K = 2
LN_EPS = 1e-5
DEN_EPS = 1e-6

CAP = TOKENS + P
DUMMY = E * CAP
BLOCKS = TOP_K * TOKENS // P + E - 1
ROW = P + 2
W_COL, DEST_COL = P, P + 1
SKIP = 1 << 20
RING = 8
PARTS = 4

C_ID = 0
C_COS = C_ID + P
C_EXPERT = C_COS + B * H
C_ECAP = C_EXPERT + E
C_HALF = C_ECAP + E
C_TURN = C_HALF + T
C_TURN_ROW = C_TURN + 1
C_END = C_TURN_ROW + 1

V_QB, V_KB, V_CQB, V_CKB, V_GAMMA, V_END = range(6)

T_ROW, T_EXPERT = range(2)


def constants():
    f = np.zeros((P, C_END), np.float32)
    f[:, C_ID:C_ID + P] = np.eye(P)
    for gap in range(B):
        for h in range(H):
            f[h * D:(h + 1) * D, C_COS + gap * H + h] = np.cos(np.pi / 2 * gap / B)
    f[:, C_EXPERT:C_EXPERT + E] = np.arange(E)
    f[:, C_ECAP:C_ECAP + E] = np.arange(E) * CAP
    f[:, C_HALF:C_HALF + T] = -0.5
    f[:, C_TURN] = np.arange(P)
    f[:, C_TURN_ROW] = np.arange(P) * P
    before = np.triu(np.ones((P, P), np.float32), 1)
    both = np.concatenate([before, np.ones((P, P), np.float32)], axis=1)
    dest = (np.arange(TOP_K)[None, None, :] * TOKENS + np.arange(P)[:, None, None] * NT
            + np.arange(NT)[None, :, None])
    return f, both, dest.reshape(P, NT * TOP_K).astype(np.int32)


def hybrid_block(nc, x_ch, x_tok, w_conv, w_lin, w_router, w13, w2, vecs, bias_rows, cst_f, cst_tri, cst_dest,
                 out):
    ctx = ExitStack()
    with ctx:
        def sb(name, shape, dt=F32):
            return ctx.enter_context(nc.sbuf_tensor(name, shape, dt))

        def sem(name):
            return ctx.enter_context(nc.semaphore(name))

        rows_x = nc.dram_tensor("rows_x", [E * CAP + P, ROW], F32, kind="Internal").ap()
        rows_y = nc.dram_tensor("rows_y", [TOP_K * TOKENS, P], F32, kind="Internal").ap()

        X = sb("X", [P, B, N])
        XT = sb("XT", [P, B, T, P])
        WC = sb("WC", [P, 2 * (PROJ + 1) + P])
        WL = sb("WL", [P, 4 * P])
        WR = sb("WR", [P, E])
        W13 = sb("W13", [P, E * 2 * F])
        W2 = sb("W2", [P, E * FK * P])
        VEC = sb("VEC", [P, V_END])
        BR = sb("BR", [65, 2 * P])
        CF = sb("CF", [P, C_END])
        TRI32 = sb("TRI32", [P, 2 * P])
        TRI = sb("TRI", [P, 2 * P], BF16)
        DEST = sb("DEST", [P, NT * TOP_K], I32)
        wq, wk, wv = WC[:, 0:PROJ + 1], WC[:, PROJ + 1:2 * PROJ + 2], WC[:, 2 * PROJ + 2:]
        lq, lk, lv, lo = (WL[:, n * P:(n + 1) * P] for n in range(4))
        ident = CF[:, C_ID:C_ID + P]

        b_part = [sb(f"b_part{n}", [65, 2 * P], BF16) for n in range(3)]
        b_rest = [sb(f"b_rest{n}", [65, 2 * P]) for n in range(2)]
        BIAS = sb("BIAS", [65, 2 * P], BF16)
        ONES = sb("ONES", [65, P], BF16)
        vb_row, ob_row = BIAS[:, 0:P], BIAS[:, P:2 * P]
        cqb8 = sb("cqb8", [PROJ + 1, 1])

        cq = sb("cq", [PROJ + 1, 2, N])
        ck = sb("ck", [PROJ + 1, 2, N])
        cv = sb("cv", [P, 2, T, P])
        nmax = sb("nmax", [P, 2, T])
        rsum = sb("rsum", [P, 2, T])
        rinv = sb("rinv", [P, T])
        gsc = sb("gsc", [P, T])
        prob = sb("prob", [P, T, N])
        probT = sb("probT", [P, T, N])
        t1 = sb("t1", [P, 2, T, P])
        st1 = sb("st1", [P, T, 6])
        mv1 = sb("mv1", [P, T, 2])
        ve1 = sb("ve1", [P, T])
        rs1 = sb("rs1", [P, T])
        xn = sb("xn", [P, T, P])
        xnT = sb("xnT", [P, N])
        qT = sb("qT", [P, N])
        kT = sb("kT", [P, B, N])
        vt = sb("vt", [P, B, T * P])
        qk = sb("qk", [P, B, N])
        den = sb("den", [P, T * H])
        denm = sb("denm", [P, T * H])
        dinv = sb("dinv", [P, T * H])
        sco = sb("sco", [P, B, T * H])
        num = sb("num", [P, B, T * P])
        attT = sb("attT", [P, N])
        t2 = sb("t2", [P, NT, P])
        st2 = sb("st2", [P, T, 6])
        mv2 = sb("mv2", [P, T, 2])
        ve2 = sb("ve2", [P, T])
        rs2 = sb("rs2", [P, T])
        xrow = sb("xrow", [P, NT, TOP_K, ROW])
        x2T = sb("x2T", [P, N])
        top = sb("top", [P, T, 8])
        topi = sb("topi", [P, T, 8], U32)
        gap = sb("gap", [P, T])
        eg = sb("eg", [P, T])
        eg1 = sb("eg1", [P, T])
        wfirst = sb("wfirst", [P, T])
        chosen = sb("chosen", [P, T, TOP_K])
        mask = sb("mask", [P, T * TOP_K, E])
        hits = sb("hits", [P, T, E], BF16)
        seen = sb("seen", [P, NT + 1, E], BF16)
        base = sb("base", [P, T, E])
        where = sb("where", [P, T * TOP_K, E])
        slot = sb("slot", [P, NT * TOP_K], I32)
        cnt = sb("cnt", [P, E])
        pad_row = sb("pad_row", [1, E], I32)
        up = sb("up", [P, E], I32)
        nbi = sb("nbi", [P, E], I32)
        nblk = sb("nblk", [P, E])
        one8 = sb("one8", [P, E])
        ends = sb("ends", [P, E])
        past = sb("past", [BLOCKS, E])
        skipped = sb("skipped", [BLOCKS, E])
        exp_f = sb("exp_f", [BLOCKS, 1])
        first_f = sb("first_f", [BLOCKS, 1])
        rel_f = sb("rel_f", [BLOCKS, 1])
        row_f = sb("row_f", [BLOCKS, 1])
        steer = sb("steer", [BLOCKS, 2])
        table = sb("table", [2, BLOCKS], I32)
        pad = sb("pad", [P, ROW])
        xb = sb("xb", [P, RING, ROW])
        xbT = sb("xbT", [P, 3, P])
        gate = sb("gate", [P, 2, F])
        hid = sb("hid", [P, 2, F])
        hidT = sb("hidT", [P, 2, FK, P])
        yb = sb("yb", [P, RING, P])
        y1 = sb("y1", [P, NT, P])
        y2 = sb("y2", [P, NT, P])

        ps = ctx.enter_context(nc.psum_tensor("ps", [P, 8, 512], F32))
        bank = lambda n: ps[:, n, :]
        ps_cqk = bank(0).rearrange("p (a n) -> p a n", a=2)
        ps_pT = bank(0).rearrange("p (k m) -> p k m", k=T)
        ps_sim = bank(1).rearrange("p (t n) -> p t n", t=T)
        ps_cv = bank(2)[:, 0:T * P].rearrange("p (t c) -> p t c", t=T)
        ps_co = bank(2)[:, T * P:2 * T * P].rearrange("p (t c) -> p t c", t=T)
        ps_xT = bank(3)[:, 0:N]
        ps_aT = bank(3)[:, N:2 * N]
        ps_qk = bank(4).rearrange("p (a n) -> p a n", a=2)
        ps_v = bank(5)[:, 0:T * P].rearrange("p (t c) -> p t c", t=T)
        ps_y = bank(5)[:, T * P:2 * T * P].rearrange("p (t c) -> p t c", t=T)
        ps_sc = bank(6)[:, 0:B * T * H].rearrange("p (j g) -> p j g", j=B)
        ps_x2T = bank(7)[:, 0:N]
        ps_log = bank(7)[:, N:N + T * E].rearrange("p (t e) -> p t e", t=T)
        ps_rank = bank(7)[:, N + T * E:N + 2 * T * E].rearrange("p (t e) -> p t e", t=T)
        ps_cnt = bank(7)[:, N + 2 * T * E:N + 2 * T * E + E]
        ps_table = bank(7)[0:2, N + 2 * T * E + E:N + 2 * T * E + E + BLOCKS]
        ps_xbT = bank(0)[:, 0:P]
        ps_hT = bank(1)[:, 0:FK * P].rearrange("p (k s) -> p k s", k=FK)
        ps_yb = bank(2)[:, 0:P]
        ps_gu = [bank(3 + n) for n in range(2)]

        ld_conv = sem("ld_conv")
        ld_x = [sem(f"ld_x{i}") for i in range(B)]
        ld_vec = sem("ld_vec")
        ld_bias = sem("ld_bias")
        ld_tri = sem("ld_tri")
        ld_dest = sem("ld_dest")
        ld_lin = sem("ld_lin")
        ld_cst = sem("ld_cst")
        ld_w13 = sem("ld_w13")
        bias_ready = sem("bias_ready")
        tri_ready = sem("tri_ready")
        cqb_ready = sem("cqb_ready")
        dest_ready = sem("dest_ready")
        pad_ready = sem("pad_ready")
        cqk_done = sem("cqk_done")
        cqk_read = sem("cqk_read")
        cv_done = sem("cv_done")
        cv_read = sem("cv_read")
        sim_done = sem("sim_done")
        max_done = sem("max_done")
        exp_done = sem("exp_done")
        pT_done = sem("pT_done")
        pT_read = sem("pT_read")
        co_done = sem("co_done")
        t1_done = sem("t1_done")
        ve1_done = sem("ve1_done")
        rs1_done = sem("rs1_done")
        xn_done = sem("xn_done")
        xT_done = sem("xT_done")
        xT_read = sem("xT_read")
        lqk_done = sem("lqk_done")
        lqk_read = sem("lqk_read")
        lv_done = sem("lv_done")
        lv_read = sem("lv_read")
        qk_done = sem("qk_done")
        sc_done = sem("sc_done")
        sco_done = sem("sco_done")
        att_done = sem("att_done")
        aT_done = sem("aT_done")
        aT_read = sem("aT_read")
        y_done = sem("y_done")
        t2_done = sem("t2_done")
        ve2_done = sem("ve2_done")
        rs2_done = sem("rs2_done")
        xrow_done = sem("xrow_done")
        x2T_done = sem("x2T_done")
        x2T_read = sem("x2T_read")
        log_done = sem("log_done")
        gap_done = sem("gap_done")
        eg_done = sem("eg_done")
        w_done = sem("w_done")
        hits_done = sem("hits_done")
        rank_done = sem("rank_done")
        slot_done = sem("slot_done")
        scattered = sem("scattered")
        cnt_done = sem("cnt_done")
        pad_row_done = sem("pad_row_done")
        steer_done = sem("steer_done")
        table_turned = sem("table_turned")
        table_done = sem("table_done")
        pads_stored = sem("pads_stored")
        dve = sem("dve")
        xb_loaded = [sem(f"xb_loaded{n}") for n in range(RING)]
        xbT_done = sem("xbT_done")
        xbT_read = sem("xbT_read")
        gu_done = sem("gu_done")
        gate_done = sem("gate_done")
        hid_done = sem("hid_done")
        hT_done = sem("hT_done")
        hT_read = sem("hT_read")
        yb_done_pe = sem("yb_done_pe")
        yb_done = sem("yb_done")
        yb_stored = [sem(f"yb_stored{n}") for n in range(RING)]
        y_loaded = [sem(f"y_loaded{n}") for n in range(4)]
        sum_done = sem("sum_done")
        out_stored = sem("out_stored")

        block = ctx.enter_context(nc.Block())
        rows_y_v = rows_y.rearrange("(c p t) d -> c p t d", c=TOP_K, p=P)

        def pad_lists(eng, experts):
            eng.wait_ge(pad_row_done, 1)
            rows = [eng.value_load(pad_row[0:1, e:e + 1], min_val=0, max_val=DUMMY - P) for e in experts]
            for row in rows:
                eng.dma_start(rows_x[bass.ds(row, P), :], pad[:, :]).then_inc(pads_stored, 16)

        def table_reader(eng, line, most):
            sets = [[eng.alloc_register(f"line{line}_{half}_{n}") for n in range(RING)] for half in range(2)]

            def read(s):
                held = sets[s // RING % 2]
                if s % RING == 0:
                    m = min(RING, BLOCKS - s)
                    eng.reg_load(held[0:m], table[line:line + 1, s:s + m])
                return eng.snap(held[s % RING], min_val=0, max_val=most)
            return read

        @block.sync
        def _(sp):
            sp.dma_start(X[:, 0, :], x_ch[:, 0, :]).then_inc(ld_x[0], 16)
            sp.dma_start(WC[:, :], w_conv).then_inc(ld_conv, 16)
            sp.dma_start(VEC[:, :], vecs).then_inc(ld_vec, 16)
            sp.dma_start(CF[:, :], cst_f).then_inc(ld_cst, 16)
            sp.dma_start(XT[:, 0, :, :], x_tok[:, 0, :, :]).then_inc(ld_x[0], 16)
            sp.dma_start(BR[:, :], bias_rows).then_inc(ld_bias, 16)
            sp.dma_start(WL[:, :], w_lin).then_inc(ld_lin, 16)
            sp.dma_start(WR[:, :], w_router).then_inc(ld_lin, 16)
            sp.dma_start(TRI32[:, :], cst_tri).then_inc(ld_tri, 16)
            sp.dma_start(DEST[:, :], cst_dest).then_inc(ld_dest, 16)
            for i in range(1, B):
                sp.dma_start(X[:, i, :], x_ch[:, i, :]).then_inc(ld_x[i], 16)
                sp.dma_start(XT[:, i, :, :], x_tok[:, i, :, :]).then_inc(ld_x[i], 16)
            sp.dma_start(W13[:, :], w13).then_inc(ld_w13, 16)
            sp.dma_start(W2[:, :], w2).then_inc(ld_w13, 16)

            sp.wait_ge(pad_ready, 2)
            sp.dma_start(rows_x[DUMMY:DUMMY + P, :], pad[:, :]).then_inc(pads_stored, 16)
            pad_lists(sp, range(0, E, 2))
            sp.wait_ge(table_done, 1)
            first_row = table_reader(sp, T_ROW, DUMMY)
            row = first_row(0)
            sp.wait_ge(pads_stored, 16 * (E + 1))
            sp.wait_ge(scattered, 16 * NT * TOP_K)
            for s in range(BLOCKS):
                if s >= RING:
                    sp.wait_ge(xbT_done, s - RING + 1)
                    sp.wait_ge(yb_stored[s % RING], 16 * (s // RING))
                sp.dma_start(xb[:, s % RING, :], rows_x[bass.ds(row, P), :]).then_inc(xb_loaded[s % RING], 16)
                if s + 1 < BLOCKS:
                    row = first_row(s + 1)

            for n in range(RING):
                sp.wait_ge(yb_stored[n], 16 * len(range(n, BLOCKS, RING)))
            for q in range(PARTS):
                a, b = q * NT // PARTS, (q + 1) * NT // PARTS
                sp.dma_start(y1[:, a:b, :], rows_y_v[0, :, a:b, :]).then_inc(y_loaded[q], 16)
                sp.dma_start(y2[:, a:b, :], rows_y_v[1, :, a:b, :]).then_inc(y_loaded[q], 16)
            for q in range(PARTS):
                a, b = q * NT // PARTS, (q + 1) * NT // PARTS
                sp.wait_ge(sum_done, q + 1)
                sp.dma_start(out[:, a:b, :], y2[:, a:b, :]).then_inc(out_stored, 16)
            sp.wait_ge(out_stored, 16 * PARTS)

        @block.gpsimd
        def _(pool):
            pool.memset(pad[:, 0:DEST_COL], 0.0).then_inc(pad_ready, 1)
            pool.memset(pad[:, DEST_COL:ROW].bitcast(I32), SKIP).then_inc(pad_ready, 1)
            pool.wait_ge(ld_dest, 16)
            pool.tensor_copy(xrow[:, :, :, DEST_COL].bitcast(I32).rearrange("p t c -> p (t c)"),
                             DEST[:, :]).then_inc(dest_ready, 1)

            def rstd_lin(i):
                pool.wait_ge(ve1_done, i + 1)
                if i >= 1:
                    pool.wait_ge(xn_done, 2 * i)
                pool.tensor_tensor(rs1[:, :], ve1[:, :], CF[:, C_HALF:C_HALF + T], ALU.pow).then_inc(rs1_done, 1)

            def rstd_ffn(i):
                pool.wait_ge(ve2_done, i + 1)
                if i >= 1:
                    pool.wait_ge(xrow_done, 2 * i)
                pool.tensor_tensor(rs2[:, :], ve2[:, :], CF[:, C_HALF:C_HALF + T], ALU.pow).then_inc(rs2_done, 1)

            def products(i):
                pool.wait_ge(lqk_read, 2 * (i + 1))
                if i >= 1:
                    pool.wait_ge(sc_done, i)
                pool.tensor_tensor(qk[:, 0:i + 1, :], kT[:, 0:i + 1, :],
                                   qT[:, :].unsqueeze(1).broadcast_to([P, i + 1, N]), ALU.mult).then_inc(qk_done, 1)

            def scatter(i):
                pool.wait_ge(slot_done, i + 1)
                pool.wait_ge(w_done, 2 * (i + 1))
                pool.wait_ge(xrow_done, 2 * (i + 1))
                pool.wait_ge(dest_ready, 1)
                for t in range(T * i, T * i + T):
                    for c in range(TOP_K):
                        g = t * TOP_K + c
                        pool.indirect_dma_start(rows_x, bass.IndirectOffsetOnAxis(ap=slot[:, g:g + 1], axis=0),
                                                xrow[:, t, c, :], None, bounds_check=DUMMY + P - 1,
                                                oob_is_err=False).then_inc(scattered, 16)

            for step in range(B + 2):
                i, j, k = step, step - 1, step - 2
                if 0 <= j < B:
                    products(j)
                if 0 <= k < B:
                    scatter(k)
                if i < B:
                    rstd_lin(i)
                if 0 <= j < B:
                    rstd_ffn(j)

            last_row = pool.to_reg(TOP_K * TOKENS - 1)
            for s in range(BLOCKS):
                n = s % RING
                pool.wait_ge(yb_done, s + 1)
                pool.indirect_dma_start(
                    rows_y, bass.IndirectOffsetOnAxis(ap=xb[:, n, DEST_COL:ROW].bitcast(I32), axis=0),
                    yb[:, n, :], None, bounds_check=last_row, oob_is_err=False).then_inc(yb_stored[n], 16)

        @block.scalar
        def _(act):
            act.wait_ge(ld_vec, 16)
            act.mul(cqb8[:, :], VEC[0:PROJ + 1, V_CQB:V_CQB + 1], PROJ ** -0.5).then_inc(cqb_ready, 1)

            def conv_qk(i):
                b = i % 2
                act.wait_ge(cqk_done, i + 1)
                if i == 0:
                    act.wait_ge(cqb_ready, 1)
                if i >= 2:
                    act.wait_ge(sim_done, i - 1)
                    act.wait_ge(co_done, i - 1)
                act.activation(cq[:, b, :], ps_cqk[0:PROJ + 1, 0, :], ACT.Identity, bias=cqb8[:, :],
                               scale=PROJ ** -0.5).then_inc(cqk_read, 1)
                act.activation(ck[:, b, :], ps_cqk[0:PROJ + 1, 1, :], ACT.Identity,
                               bias=VEC[0:PROJ + 1, V_CKB:V_CKB + 1]).then_inc(cqk_read, 1)
                act.wait_ge(cv_done, i + 1)
                act.activation(cv[:, b, :, :], ps_cv, ACT.Copy).then_inc(cv_read, 1)

            def conv_exp(i):
                b = i % 2
                act.wait_ge(max_done, i + 1)
                if i >= 1:
                    act.wait_ge(pT_done, i)
                for t in range(T):
                    act.activation(prob[:, t, :], ps_sim[:, t, :], ACT.Exp, bias=nmax[:, b, t:t + 1],
                                   accum_out=rsum[:, b, t:t + 1]).then_inc(exp_done, 1)

            def conv_pT(i):
                act.wait_ge(pT_done, i + 1)
                if i >= 1:
                    act.wait_ge(co_done, i)
                act.activation(probT[:, :, :], ps_pT, ACT.Copy).then_inc(pT_read, 1)

            def lin_xT(i):
                act.wait_ge(xT_done, i + 1)
                if i >= 1:
                    act.wait_ge(lv_done, i)
                act.activation(xnT[:, :], ps_xT, ACT.Copy).then_inc(xT_read, 1)

            def lin_qkv(i):
                act.wait_ge(lqk_done, i + 1)
                if i >= 1:
                    act.wait_ge(qk_done, i)
                act.activation(qT[:, :], ps_qk[:, 0, :], ACT.Relu, bias=VEC[:, V_QB:V_QB + 1]).then_inc(lqk_read, 1)
                act.activation(kT[:, i, :], ps_qk[:, 1, :], ACT.Relu, bias=VEC[:, V_KB:V_KB + 1]).then_inc(lqk_read, 1)
                act.wait_ge(lv_done, i + 1)
                act.activation(vt[:, i, :].rearrange("p (t c) -> p t c", t=T), ps_v, ACT.Copy).then_inc(lv_read, 1)

            def lin_aT(i):
                act.wait_ge(aT_done, i + 1)
                if i >= 1:
                    act.wait_ge(y_done, i)
                act.activation(attT[:, :], ps_aT, ACT.Copy).then_inc(aT_read, 1)

            def route_xT(i):
                act.wait_ge(x2T_done, i + 1)
                if i >= 1:
                    act.wait_ge(log_done, i)
                act.activation(x2T[:, :], ps_x2T, ACT.Copy).then_inc(x2T_read, 1)

            def route_exp(i):
                act.wait_ge(gap_done, i + 1)
                if i >= 1:
                    act.wait_ge(w_done, 2 * i)
                act.activation(eg[:, :], gap[:, :], ACT.Exp).then_inc(eg_done, 1)

            for step in range(B + 2):
                i, j, k = step, step - 1, step - 2
                if i < B:
                    conv_qk(i)
                if 0 <= j < B:
                    lin_xT(j)
                if i < B:
                    conv_exp(i)
                if 0 <= j < B:
                    lin_qkv(j)
                if 0 <= k < B:
                    route_xT(k)
                if i < B:
                    conv_pT(i)
                if 0 <= k < B:
                    route_exp(k)
                if 0 <= j < B:
                    lin_aT(j)

            act.wait_ge(pad_ready, 2)
            pad_lists(act, range(1, E, 2))

            def turned_x(s):
                act.wait_ge(xbT_done, s + 1)
                if s >= 3:
                    act.wait_ge(gu_done, s - 2)
                act.activation(xbT[:, s % 3, :], ps_xbT, ACT.Copy).then_inc(xbT_read, 1)

            def silu(s):
                act.wait_ge(gu_done, s + 1)
                if s >= 2:
                    act.wait_ge(hid_done, s - 1)
                act.activation(gate[:, s % 2, :], ps_gu[s % 2][:, 0:F], ACT.Silu).then_inc(gate_done, 1)

            for s in range(-2, BLOCKS):
                if s + 2 < BLOCKS:
                    turned_x(s + 2)
                if 0 <= s + 1 < BLOCKS:
                    silu(s + 1)

        @block.tensor
        def _(pe):
            def conv_proj(i):
                if i == 0:
                    pe.wait_ge(ld_conv, 16)
                pe.wait_ge(ld_x[i], 32)
                if i >= 1:
                    pe.wait_ge(pT_read, i)
                pe.matmul(ps_cqk[0:PROJ + 1, 0, :], wq, X[:, i, :], start=True, stop=True)
                pe.matmul(ps_cqk[0:PROJ + 1, 1, :], wk, X[:, i, :], start=True, stop=True).then_inc(cqk_done, 1)
                if i >= 1:
                    pe.wait_ge(t1_done, 2 * i)
                for t in range(T):
                    last = pe.matmul(ps_cv[:, t, :], X[:, i, t * P:(t + 1) * P], wv, start=True, stop=True)
                last.then_inc(cv_done, 1)

            def conv_scores(i):
                b = i % 2
                pe.wait_ge(cqk_read, 2 * (i + 1))
                if i >= 1:
                    pe.wait_ge(exp_done, 2 * i)
                for t in range(T):
                    last = pe.matmul(ps_sim[:, t, :], cq[:, b, t * P:(t + 1) * P], ck[:, b, :], start=True, stop=True)
                last.then_inc(sim_done, 1)

            def conv_turn(i):
                if i == 0:
                    pe.wait_ge(ld_cst, 16)
                pe.wait_ge(exp_done, 2 * (i + 1))
                for k in range(T):
                    for t in range(T):
                        last = pe.transpose(ps_pT[:, k, t * P:(t + 1) * P], prob[:, t, k * P:(k + 1) * P], ident)
                last.then_inc(pT_done, 1)

            def conv_out(i):
                b = i % 2
                pe.wait_ge(pT_read, i + 1)
                pe.wait_ge(cv_read, i + 1)
                for t in range(T):
                    for k in range(T):
                        last = pe.matmul(ps_co[:, t, :], probT[:, k, t * P:(t + 1) * P], cv[:, b, k, :],
                                         start=(k == 0), stop=(k == T - 1))
                last.then_inc(co_done, 1)

            def lin_turn(i):
                pe.wait_ge(xn_done, 2 * (i + 1))
                if i >= 1:
                    pe.wait_ge(aT_read, i)
                for t in range(T):
                    last = pe.transpose(ps_xT[:, t * P:(t + 1) * P], xn[:, t, :], ident)
                last.then_inc(xT_done, 1)

            def lin_proj(i):
                if i == 0:
                    pe.wait_ge(ld_lin, 32)
                    pe.wait_ge(bias_ready, 1)
                pe.wait_ge(xT_read, i + 1)
                if i >= 1:
                    pe.wait_ge(lqk_read, 2 * i)
                pe.matmul(ps_qk[:, 0, :], lq, xnT[:, :], start=True, stop=True)
                pe.matmul(ps_qk[:, 1, :], lk, xnT[:, :], start=True, stop=True).then_inc(lqk_done, 1)
                if i >= 1:
                    pe.wait_ge(t2_done, i)
                for t in range(T):
                    pe.matmul(ps_v[:, t, :], xnT[:, t * P:(t + 1) * P], lv, start=True, stop=False)
                    last = pe.matmul(ps_v[:, t, :], ONES[:, :], vb_row, start=False, stop=True)
                last.then_inc(lv_done, 1)

            def lin_scores(i):
                pe.wait_ge(qk_done, i + 1)
                if i >= 1:
                    pe.wait_ge(sco_done, i)
                for j in range(i + 1):
                    heads = CF[:, C_COS + (i - j) * H:C_COS + (i - j + 1) * H]
                    for t in range(T):
                        last = pe.matmul(ps_sc[:, j, t * H:(t + 1) * H], qk[:, j, t * P:(t + 1) * P], heads,
                                         start=True, stop=True)
                last.then_inc(sc_done, 1)

            def lin_out_turn(i):
                pe.wait_ge(att_done, i + 1)
                for t in range(T):
                    last = pe.transpose(ps_aT[:, t * P:(t + 1) * P], num[:, 0, t * P:(t + 1) * P], ident)
                last.then_inc(aT_done, 1)

            def lin_out(i):
                pe.wait_ge(aT_read, i + 1)
                pe.wait_ge(lv_read, i + 1)
                for t in range(T):
                    pe.matmul(ps_y[:, t, :], attT[:, t * P:(t + 1) * P], lo, start=True, stop=False)
                    last = pe.matmul(ps_y[:, t, :], ONES[:, :], ob_row, start=False, stop=True)
                last.then_inc(y_done, 1)

            def route_turn(i):
                pe.wait_ge(xrow_done, 2 * (i + 1))
                if i >= 1:
                    pe.wait_ge(slot_done, i)
                for t in range(T):
                    last = pe.transpose(ps_x2T[:, t * P:(t + 1) * P], xrow[:, i * T + t, 0, 0:P], ident)
                last.then_inc(x2T_done, 1)

            def route_logits(i):
                pe.wait_ge(x2T_read, i + 1)
                for t in range(T):
                    last = pe.matmul(ps_log[:, t, :], x2T[:, t * P:(t + 1) * P], WR[:, :], start=True, stop=True)
                last.then_inc(log_done, 1)

            def route_rank(i):
                pe.wait_ge(hits_done, 3 * (i + 1))
                pe.wait_ge(tri_ready, 1)
                for t in range(T):
                    pe.matmul(ps_rank[:, t, :], TRI[:, 0:P], hits[:, t, :], start=True, stop=False)
                    last = pe.matmul(ps_rank[:, t, :], TRI[:, P:2 * P], seen[:, i * T + t, :], start=False, stop=True)
                last.then_inc(rank_done, 1)

            for step in range(B + 2):
                i, j, k = step, step - 1, step - 2
                if i < B:
                    conv_proj(i)
                if 0 <= j < B:
                    lin_turn(j)
                if i < B:
                    conv_scores(i)
                if 0 <= j < B:
                    lin_proj(j)
                if 0 <= k < B:
                    route_turn(k)
                    route_logits(k)
                if i < B:
                    conv_turn(i)
                if 0 <= j < B:
                    lin_scores(j)
                if 0 <= k < B:
                    route_rank(k)
                if i < B:
                    conv_out(i)
                if 0 <= j < B:
                    lin_out_turn(j)
                    lin_out(j)

            pe.wait_ge(slot_done, B)
            pe.matmul(ps_cnt, TRI[:, P:2 * P], seen[:, NT, :], start=True, stop=True).then_inc(cnt_done, 1)
            pe.wait_ge(steer_done, 2)
            pe.transpose(ps_table, steer[:, :], CF[0:BLOCKS, C_ID:C_ID + BLOCKS]).then_inc(table_turned, 1)

            def turn_x(s):
                if s >= 1:
                    pe.wait_ge(xbT_read, s)
                pe.wait_ge(xb_loaded[s % RING], 16 * (s // RING + 1))
                pe.transpose(ps_xbT, xb[:, s % RING, 0:P], ident).then_inc(xbT_done, 1)

            def gate_up(s, e):
                if s >= 2:
                    pe.wait_ge(hid_done, s - 1)
                pe.wait_ge(xbT_read, s + 1)
                pe.matmul(ps_gu[s % 2], xbT[:, s % 3, :], W13[:, bass.ds(e * (2 * F), 2 * F)], start=True, stop=True)\
                  .then_inc(gu_done, 1)

            def down(s, e):
                if s >= 1:
                    pe.wait_ge(yb_done, s)
                pe.wait_ge(hT_read, s + 1)
                for k in range(FK):
                    last = pe.matmul(ps_yb, hidT[:, s % 2, k, :], W2[:, bass.ds(e * (FK * P) + k * P, P)],
                                     start=(k == 0), stop=(k == FK - 1))
                last.then_inc(yb_done_pe, 1)

            def turn_h(s):
                if s >= 1:
                    pe.wait_ge(hT_read, s)
                pe.wait_ge(hid_done, s + 1)
                for k in range(FK):
                    last = pe.transpose(ps_hT[:, k, :], hid[:, s % 2, k * P:(k + 1) * P], ident)
                last.then_inc(hT_done, 1)

            pe.wait_ge(ld_w13, 32)
            pe.wait_ge(table_done, 1)
            expert = table_reader(pe, T_EXPERT, E - 1)
            experts = [expert(0)]
            for s in range(-2, BLOCKS + 1):
                if s + 2 < BLOCKS:
                    turn_x(s + 2)
                if 0 <= s + 1 < BLOCKS:
                    gate_up(s + 1, experts[s + 1])
                    if s + 2 < BLOCKS:
                        experts.append(expert(s + 2))
                if 0 <= s - 1:
                    down(s - 1, experts[s - 1])
                if 0 <= s < BLOCKS:
                    turn_h(s)

        @block.vector
        def _(dv):
            links = [0]

            def link(ins):
                links[0] += 1
                ins.then_inc(dve, 1)
                dv.wait_ge(dve, links[0])

            dv.memset(ONES[:, :], 1.0)
            link(dv.memset(BIAS[:, :], 0.0))
            dv.memset(seen[:, 0, :], 0.0)
            dv.memset(one8[:, :], 1.0)
            dv.wait_ge(ld_bias, 16)
            link(dv.tensor_copy(b_part[0][:, :], BR[:, :]))
            link(dv.tensor_tensor(b_rest[0][:, :], BR[:, :], b_part[0][:, :], ALU.subtract))
            link(dv.tensor_copy(b_part[1][:, :], b_rest[0][:, :]))
            link(dv.tensor_tensor(b_rest[1][:, :], b_rest[0][:, :], b_part[1][:, :], ALU.subtract))
            link(dv.tensor_copy(b_part[2][:, :], b_rest[1][:, :]))
            for n in range(3):
                last = dv.tensor_copy(BIAS[32 * n:32 * n + 1, :], b_part[n][32 * n:32 * n + 1, :])
                if n < 2:
                    link(last)
            last.then_inc(bias_ready, 1)
            dv.wait_ge(ld_tri, 16)
            dv.tensor_copy(TRI[:, :], TRI32[:, :]).then_inc(tri_ready, 1)
            dv.wait_ge(ld_vec, 16)
            dv.wait_ge(ld_cst, 16)

            def conv_max(i):
                dv.wait_ge(sim_done, i + 1)
                if i >= 2:
                    dv.wait_ge(exp_done, 2 * (i - 1))
                dv.tensor_reduce(nmax[:, i % 2, :], ps_sim, AX.X, ALU.max, negate=True).then_inc(max_done, 1)

            def conv_add(i):
                b = i % 2
                dv.wait_ge(exp_done, 2 * (i + 1))
                link(dv.reciprocal(rinv[:, :], rsum[:, b, :]))
                link(dv.tensor_scalar(gsc[:, :], rinv[:, :], VEC[:, V_GAMMA:V_GAMMA + 1], None, ALU.mult))
                dv.wait_ge(co_done, i + 1)
                dv.wait_ge(ld_x[i], 32)
                if i >= 2:
                    dv.wait_ge(t2_done, i - 1)
                for t in range(T):
                    last = dv.scalar_tensor_tensor(out=t1[:, b, t, :], in0=ps_co[:, t, :], scalar=gsc[:, t:t + 1],
                                                   in1=XT[:, i, t, :], op0=ALU.mult, op1=ALU.add)
                    last.then_inc(t1_done, 1)
                dv.wait_ge(t1_done, 2 * (i + 1))
                if i >= 1:
                    dv.wait_ge(rs1_done, i)
                norm_stats(t1[:, b, :, :], st1, mv1, ve1, ve1_done)

            def norm_stats(x, st, mv, ve, done):
                for t in range(T):
                    last = dv.bn_stats(st[:, t, :], x[:, t, :])
                link(last)
                for t in range(T):
                    last = dv.bn_aggr(mv[:, t, :], st[:, t, :])
                link(last)
                dv.tensor_scalar(ve[:, :], mv[:, :, 1], LN_EPS, None, ALU.add).then_inc(done, 1)

            def lin_norm(i):
                dv.wait_ge(rs1_done, i + 1)
                if i >= 1:
                    dv.wait_ge(xT_done, i)
                for t in range(T):
                    dv.tensor_scalar(xn[:, t, :], t1[:, i % 2, t, :], mv1[:, t, 0:1], rs1[:, t:t + 1],
                                     ALU.subtract, ALU.mult).then_inc(xn_done, 1)

            def lin_weights(i):
                dv.wait_ge(sc_done, i + 1)
                sc = ps_sc[:, 0:i + 1, :]
                link(dv.tensor_reduce(den[:, :], sc.rearrange("p j g -> p g j"), AX.X, ALU.add))
                link(dv.tensor_scalar(denm[:, :], den[:, :], DEN_EPS, None, ALU.max))
                link(dv.reciprocal(dinv[:, :], denm[:, :]))
                dv.tensor_tensor(sco[:, 0:i + 1, :], sc, dinv[:, :].unsqueeze(1).broadcast_to([P, i + 1, T * H]),
                                 ALU.mult).then_inc(sco_done, 1)

            def lin_values(i):
                dv.wait_ge(sco_done, i + 1)
                dv.wait_ge(lv_read, i + 1)
                if i >= 1:
                    dv.wait_ge(aT_done, i)
                m = i + 1
                w = sco[:, 0:m, :].rearrange("p j g -> p (j g)").unsqueeze(2).broadcast_to([P, m * T * H, D])
                ins = dv.tensor_tensor(num[:, 0:m, :].rearrange("p j (g d) -> p (j g) d", d=D),
                                       vt[:, 0:m, :].rearrange("p j (g d) -> p (j g) d", d=D), w, ALU.mult)
                while m > 1:
                    half = m // 2
                    link(ins)
                    ins = dv.tensor_tensor(num[:, 0:half, :], num[:, 0:half, :], num[:, m - half:m, :], ALU.add)
                    m -= half
                ins.then_inc(att_done, 1)

            def lin_add(i):
                dv.wait_ge(y_done, i + 1)
                x = t2[:, i * T:(i + 1) * T, :]
                dv.tensor_tensor(x, ps_y, t1[:, i % 2, :, :], ALU.add).then_inc(t2_done, 1)
                dv.wait_ge(t2_done, i + 1)
                if i >= 1:
                    dv.wait_ge(rs2_done, i)
                norm_stats(x, st2, mv2, ve2, ve2_done)

            def route_norm(i):
                dv.wait_ge(rs2_done, i + 1)
                for t in range(T):
                    dv.tensor_scalar(xrow[:, i * T + t, :, 0:P],
                                     t2[:, i * T + t, :].unsqueeze(1).broadcast_to([P, TOP_K, P]),
                                     mv2[:, t, 0:1], rs2[:, t:t + 1], ALU.subtract, ALU.mult).then_inc(xrow_done, 1)

            def route_top(i):
                dv.wait_ge(log_done, i + 1)
                for t in range(T):
                    last = dv.max(top[:, t, :], ps_log[:, t, :])
                link(last)
                for t in range(T):
                    last = dv.max_index(topi[:, t, :], top[:, t, :], ps_log[:, t, :])
                if i >= 1:
                    dv.wait_ge(eg_done, i)
                dv.tensor_tensor(gap[:, :], top[:, :, 1], top[:, :, 0], ALU.subtract).then_inc(gap_done, 1)
                link(last)
                link(dv.tensor_copy(chosen[:, :, :], topi[:, :, 0:TOP_K]))
                g = T * TOP_K
                link(dv.tensor_tensor(mask[:, :, :],
                                      CF[:, C_EXPERT:C_EXPERT + E].unsqueeze(1).broadcast_to([P, g, E]),
                                      chosen[:, :, :].rearrange("p t c -> p (t c)").unsqueeze(2).broadcast_to([P, g, E]),
                                      ALU.is_equal))
                m = mask[:, :, :].rearrange("p (t c) e -> p t c e", c=TOP_K)
                if i >= 1:
                    dv.wait_ge(rank_done, i)
                dv.tensor_tensor(hits[:, :, :], m[:, :, 0, :], m[:, :, 1, :], ALU.add).then_inc(hits_done, 1)
                dv.wait_ge(hits_done, 3 * i + 1)
                for t in range(T):
                    n = i * T + t
                    dv.tensor_tensor(seen[:, n + 1, :], seen[:, n, :], hits[:, t, :], ALU.add).then_inc(hits_done, 1)
                    dv.wait_ge(hits_done, 3 * i + 2 + t)

            def route_weights(i):
                dv.wait_ge(eg_done, i + 1)
                link(dv.tensor_scalar(eg1[:, :], eg[:, :], 1.0, None, ALU.add))
                link(dv.reciprocal(wfirst[:, :], eg1[:, :]))
                tiles = xrow[:, i * T:(i + 1) * T, :, :]
                dv.tensor_copy(tiles[:, :, 0, W_COL], wfirst[:, :]).then_inc(w_done, 1)
                dv.tensor_tensor(tiles[:, :, 1, W_COL], eg[:, :], wfirst[:, :], ALU.mult).then_inc(w_done, 1)

            def route_slots(i):
                dv.wait_ge(rank_done, i + 1)
                link(dv.tensor_tensor(base[:, :, :], ps_rank,
                                      CF[:, C_ECAP:C_ECAP + E].unsqueeze(1).broadcast_to([P, T, E]), ALU.add))
                link(dv.tensor_tensor(where[:, :, :].rearrange("p (t c) e -> p t c e", c=TOP_K),
                                      mask[:, :, :].rearrange("p (t c) e -> p t c e", c=TOP_K),
                                      base[:, :, :].unsqueeze(2).broadcast_to([P, T, TOP_K, E]), ALU.mult))
                g = T * TOP_K
                with nc.allow_low_precision(reason="whole numbers below 2 ** 24, summed in float32"):
                    dv.tensor_reduce(slot[:, i * g:(i + 1) * g], where[:, :, :], AX.X, ALU.add).then_inc(slot_done, 1)

            for step in range(B + 2):
                i, j, k = step, step - 1, step - 2
                if 0 <= j < B:
                    lin_norm(j)
                if 0 <= k < B:
                    route_norm(k)
                if i < B:
                    conv_max(i)
                if 0 <= k < B:
                    route_top(k)
                if 0 <= j < B:
                    lin_weights(j)
                if 0 <= k < B:
                    route_weights(k)
                    route_slots(k)
                if 0 <= j < B:
                    lin_values(j)
                if i < B:
                    conv_add(i)
                if 0 <= j < B:
                    lin_add(j)

            dv.wait_ge(cnt_done, 1)
            link(dv.tensor_copy(cnt[:, :], ps_cnt))
            dv.tensor_tensor(pad_row[:, :], cnt[0:1, :], CF[0:1, C_ECAP:C_ECAP + E], ALU.add).then_inc(pad_row_done, 1)
            link(dv.tensor_scalar(up[:, :], cnt[:, :], float(P - 1), None, ALU.add))
            link(dv.tensor_scalar(nbi[:, :], up[:, :], P.bit_length() - 1, None, ALU.logical_shift_right))
            link(dv.tensor_copy(nblk[:, :], nbi[:, :]))
            link(dv.tensor_tensor_scan(ends[:, :], one8[:, :], nblk[:, :], 0.0, ALU.mult, ALU.add))
            link(dv.tensor_scalar(past[:, :], ends[0:BLOCKS, :], CF[0:BLOCKS, C_TURN:C_TURN + 1], None, ALU.is_le))
            link(dv.tensor_tensor(skipped[:, :], past[:, :], nblk[0:BLOCKS, :], ALU.mult))
            link(dv.tensor_reduce(exp_f[:, :], past[:, :], AX.X, ALU.add))
            link(dv.tensor_reduce(first_f[:, :], skipped[:, :], AX.X, ALU.add))
            link(dv.tensor_scalar(rel_f[:, :], first_f[:, :], -float(P), CF[0:BLOCKS, C_TURN_ROW:C_TURN_ROW + 1],
                                  ALU.mult, ALU.add))
            link(dv.scalar_tensor_tensor(out=row_f[:, :], in0=exp_f[:, :], scalar=float(CAP), in1=rel_f[:, :],
                                         op0=ALU.mult, op1=ALU.add))
            dv.tensor_scalar(steer[:, T_ROW:T_ROW + 1], row_f[:, :], float(DUMMY), None, ALU.min).then_inc(steer_done, 1)
            dv.tensor_scalar(steer[:, T_EXPERT:T_EXPERT + 1], exp_f[:, :], float(E - 1), None, ALU.min)\
              .then_inc(steer_done, 1)
            dv.wait_ge(table_turned, 1)
            dv.tensor_copy(table[:, :], ps_table).then_inc(table_done, 1)

            def hidden(s):
                dv.wait_ge(gate_done, s + 1)
                if s >= 2:
                    dv.wait_ge(hT_done, s - 1)
                dv.tensor_tensor(hid[:, s % 2, :], gate[:, s % 2, :], ps_gu[s % 2][:, F:2 * F], ALU.mult)\
                  .then_inc(hid_done, 1)

            def hidden_T(s):
                dv.wait_ge(hT_done, s + 1)
                if s >= 2:
                    dv.wait_ge(yb_done_pe, s - 1)
                dv.tensor_copy(hidT[:, s % 2, :, :], ps_hT).then_inc(hT_read, 1)

            def weigh(s):
                n = s % RING
                dv.wait_ge(yb_done_pe, s + 1)
                if s >= RING:
                    dv.wait_ge(yb_stored[n], 16 * (s // RING))
                dv.tensor_scalar(yb[:, n, :], ps_yb, xb[:, n, W_COL:W_COL + 1], None, ALU.mult).then_inc(yb_done, 1)

            hidden(0)
            for s in range(BLOCKS + 1):
                if s >= 1:
                    weigh(s - 1)
                if s < BLOCKS:
                    hidden_T(s)
                if s + 1 < BLOCKS:
                    hidden(s + 1)

            for q in range(PARTS):
                a, b = q * NT // PARTS, (q + 1) * NT // PARTS
                dv.wait_ge(y_loaded[q], 32)
                link(dv.tensor_tensor(y1[:, a:b, :], y1[:, a:b, :], t2[:, a:b, :], ALU.add))
                dv.tensor_tensor(y2[:, a:b, :], y1[:, a:b, :], y2[:, a:b, :], ALU.add).then_inc(sum_done, 1)


def kernel(x, L0_conv_wq, L0_conv_bq, L0_conv_wk, L0_conv_bk, L0_conv_wv, L0_conv_wkm, L0_conv_bkm, L0_conv_gamma,
           L1_attn_q_w, L1_attn_q_b, L1_attn_k_w, L1_attn_k_b, L1_attn_v_w, L1_attn_v_b, L1_attn_out_w,
           L1_attn_out_b, L1_ffn_router_w, L1_ffn_w1, L1_ffn_w2, L1_ffn_w3):
    import concourse.bacc as bacc
    from concourse.bass_utils import run_bass_kernel_spmd

    x3 = np.asarray(x).reshape(B, P, N)
    zero_col = np.zeros((P, 1), np.float32)
    vecs = np.zeros((P, V_END), np.float32)
    vecs[:, V_QB], vecs[:, V_KB] = L1_attn_q_b, L1_attn_k_b
    vecs[0:PROJ, V_CQB], vecs[PROJ, V_CQB] = L0_conv_bq, PROJ ** 0.5
    vecs[0:PROJ, V_CKB], vecs[PROJ, V_CKB] = L0_conv_bk, L0_conv_bkm[0]
    vecs[:, V_GAMMA] = L0_conv_gamma[0]
    bias_rows = np.zeros((65, 2 * P), np.float32)
    bias_rows[::32] = np.concatenate([L1_attn_v_b, L1_attn_out_b])
    cst_f, cst_tri, cst_dest = constants()
    w13 = np.concatenate([L1_ffn_w1, L1_ffn_w3], axis=2)
    arrays = {
        "x_ch": x3.transpose(1, 0, 2),
        "x_tok": x3.reshape(B, P, T, P).transpose(3, 0, 2, 1),
        "w_conv": np.concatenate([np.asarray(L0_conv_wq).T, zero_col, np.asarray(L0_conv_wk).T,
                                  np.asarray(L0_conv_wkm).T, np.asarray(L0_conv_wv).T], axis=1),
        "w_lin": np.concatenate([np.asarray(w).T for w in (L1_attn_q_w, L1_attn_k_w, L1_attn_v_w, L1_attn_out_w)],
                                axis=1),
        "w_router": np.asarray(L1_ffn_router_w),
        "w13": w13.transpose(1, 0, 2).reshape(P, E * 2 * F),
        "w2": np.asarray(L1_ffn_w2).reshape(E, FK, P, P).transpose(2, 0, 1, 3).reshape(P, E * FK * P),
        "vecs": vecs,
        "bias_rows": bias_rows,
        "cst_f": cst_f,
        "cst_tri": cst_tri,
        "cst_dest": cst_dest,
    }
    arrays = {f"in_{n}": np.ascontiguousarray(a) for n, a in arrays.items()}
    nc = bacc.Bacc("TRN2", target_bir_lowering=False, num_devices=1)
    args = [nc.dram_tensor(n, a.shape, mybir.dt.from_np(a.dtype), kind="ExternalInput").ap()
            for n, a in arrays.items()]
    args.append(nc.dram_tensor("out_tok", (P, NT, P), F32, kind="ExternalOutput").ap())
    hybrid_block(nc, *args)
    r = run_bass_kernel_spmd(nc, [arrays], core_ids=[0])
    got = r.results[0]["out_tok"]
    return got.reshape(P, B, T, P).transpose(1, 3, 2, 0).reshape(B, P, 16, 16)
```

```python
from contextlib import ExitStack

import numpy as np

import concourse.bass as bass
from concourse import mybir

ALU = mybir.AluOpType
ACT = mybir.ActivationFunctionType
AX = mybir.AxisListType
F32 = mybir.dt.float32
BF16 = mybir.dt.bfloat16
I32 = mybir.dt.int32
U32 = mybir.dt.uint32

P = 128
B = 8
N = 256
T = N // P
NT = B * T
TOKENS = B * N
PROJ = 64
H = 8
D = P // H
E = 8
F = 256
FK = F // P
TOP_K = 2
LN_EPS = 1e-5
DEN_EPS = 1e-6

CAP = TOKENS + P
DUMMY = E * CAP
BLOCKS = TOP_K * TOKENS // P + E - 1
ROW = P + 2
W_COL, DEST_COL = P, P + 1
SKIP = 1 << 20
READ = 8
RING = 12
PARTS = 6

(BANK_CQK, BANK_CV, BANK_SIM, BANK_PT, BANK_CO, BANK_XT, BANK_QK, BANK_V, BANK_AT, BANK_Y, BANK_X2T, BANK_LOG,
 BANK_RANK) = 0, 2, 1, 0, 2, 3, 4, 5, 3, 5, 7, 7, 7
BANK_SC = 6

WARM_MATMULS = 16
VECTOR_SHARE = 3
STEPS = B + 12

C_ID = 0
C_COS = C_ID + P
C_EXPERT = C_COS + B * H
C_ECAP = C_EXPERT + E
C_HALF = C_ECAP + E
C_TURN = C_HALF + T
C_TURN_ROW = C_TURN + 1
C_END = C_TURN_ROW + 1

V_QB, V_KB, V_CQB, V_CKB, V_GAMMA, V_END = range(6)

T_ROW, T_EXPERT = range(2)


def constants():
    f = np.zeros((P, C_END), np.float32)
    f[:, C_ID:C_ID + P] = np.eye(P)
    for gap in range(B):
        for h in range(H):
            f[h * D:(h + 1) * D, C_COS + gap * H + h] = np.cos(np.pi / 2 * gap / B)
    f[:, C_EXPERT:C_EXPERT + E] = np.arange(E)
    f[:, C_ECAP:C_ECAP + E] = np.arange(E) * CAP
    f[:, C_HALF:C_HALF + T] = -0.5
    f[:, C_TURN] = np.arange(P)
    f[:, C_TURN_ROW] = np.arange(P) * P
    before = np.triu(np.ones((P, P), np.float32), 1)
    both = np.concatenate([before, np.ones((P, P), np.float32)], axis=1)
    dest = (np.arange(TOP_K)[None, None, :] * TOKENS + np.arange(P)[:, None, None] * NT
            + np.arange(NT)[None, :, None])
    return f, both, dest.reshape(P, NT * TOP_K).astype(np.int32)


def hybrid_block(nc, x_ch, x_tok, w_conv, w_lin, w_router, w13, w2, vecs, bias_rows, cst_f, cst_tri, cst_dest,
                 out):
    ctx = ExitStack()
    with ctx:
        def sb(name, shape, dt=F32):
            return ctx.enter_context(nc.sbuf_tensor(name, shape, dt))

        def sem(name):
            return ctx.enter_context(nc.semaphore(name))

        rows_x = nc.dram_tensor("rows_x", [E * CAP + P, ROW], F32, kind="Internal").ap()
        rows_y = nc.dram_tensor("rows_y", [TOP_K * TOKENS, P], F32, kind="Internal").ap()

        X = sb("X", [P, B, N])
        XT = sb("XT", [P, B, T, P])
        WC = sb("WC", [P, 2 * (PROJ + 1) + P])
        WL = sb("WL", [P, 4 * P])
        WR = sb("WR", [P, E])
        W13 = sb("W13", [P, E * 2 * F])
        W2 = sb("W2", [P, E * FK * P])
        VEC = sb("VEC", [P, V_END])
        BR = sb("BR", [65, 2 * P])
        CF = sb("CF", [P, C_END])
        TRI32 = sb("TRI32", [P, 2 * P])
        TRI = sb("TRI", [P, 2 * P], BF16)
        DEST = sb("DEST", [P, NT * TOP_K], I32)
        wq, wk, wv = WC[:, 0:PROJ + 1], WC[:, PROJ + 1:2 * PROJ + 2], WC[:, 2 * PROJ + 2:]
        lq, lk, lv, lo = (WL[:, n * P:(n + 1) * P] for n in range(4))
        ident = CF[:, C_ID:C_ID + P]

        b_part = [sb(f"b_part{n}", [65, 2 * P], BF16) for n in range(3)]
        b_rest = [sb(f"b_rest{n}", [65, 2 * P]) for n in range(2)]
        BIAS = sb("BIAS", [65, 2 * P], BF16)
        ONES = sb("ONES", [65, P], BF16)
        vb_row, ob_row = BIAS[:, 0:P], BIAS[:, P:2 * P]
        cqb8 = sb("cqb8", [PROJ + 1, 1])
        warm = sb("warm", [PROJ + 1, 1])

        cq = sb("cq", [PROJ + 1, 2, N])
        ck = sb("ck", [PROJ + 1, 2, N])
        cv = sb("cv", [P, 2, T, P])
        nmax = sb("nmax", [P, 2, T])
        rsum = sb("rsum", [P, 2, T])
        rinv = sb("rinv", [P, 2, T])
        gsc = sb("gsc", [P, 2, T])
        prob = sb("prob", [P, 2, T, N])
        probT = sb("probT", [P, 2, T, N])
        t1 = sb("t1", [P, B, T, P])
        st1 = sb("st1", [P, 2, T, 6])
        mv1 = sb("mv1", [P, 2, T, 2])
        ve1 = sb("ve1", [P, 2, T])
        rs1 = sb("rs1", [P, 2, T])
        xn = sb("xn", [P, 2, T, P])
        xnT = sb("xnT", [P, 2, N])
        qT = sb("qT", [P, 2, N])
        kT = sb("kT", [P, B, N])
        vt = sb("vt", [P, B, T * P])
        qk = sb("qk", [P, 2, B, N])
        den = sb("den", [P, 2, T * H])
        denm = sb("denm", [P, 2, T * H])
        dinv = sb("dinv", [P, 2, T * H])
        sco = sb("sco", [P, 2, B, T * H])
        num = sb("num", [P, 2, B, T * P])
        attT = sb("attT", [P, 2, N])
        t2 = sb("t2", [P, NT, P])
        st2 = sb("st2", [P, 2, T, 6])
        mv2 = sb("mv2", [P, 2, T, 2])
        ve2 = sb("ve2", [P, 2, T])
        rs2 = sb("rs2", [P, 2, T])
        xrow = sb("xrow", [P, NT, TOP_K, ROW])
        x2T = sb("x2T", [P, 2, N])
        top = sb("top", [P, 2, T, 8])
        topi = sb("topi", [P, 2, T, 8], U32)
        gap = sb("gap", [P, 2, T])
        eg = sb("eg", [P, 2, T])
        eg1 = sb("eg1", [P, 2, T])
        wfirst = sb("wfirst", [P, 2, T])
        mask = sb("mask", [P, 2, T * TOP_K, E])
        hits = sb("hits", [P, 2, T, E], BF16)
        seen = sb("seen", [P, NT + 1, E], BF16)
        base = sb("base", [P, 2, T, E])
        where = sb("where", [P, 2, T * TOP_K, E])
        slot = sb("slot", [P, NT * TOP_K], I32)
        cnt = sb("cnt", [P, E])
        pad_row = sb("pad_row", [1, E], I32)
        up = sb("up", [P, E], I32)
        nbi = sb("nbi", [P, E], I32)
        nblk = sb("nblk", [P, E])
        one8 = sb("one8", [P, E])
        ends = sb("ends", [P, E])
        past = sb("past", [BLOCKS, E])
        skipped = sb("skipped", [BLOCKS, E])
        exp_f = sb("exp_f", [BLOCKS, 1])
        first_f = sb("first_f", [BLOCKS, 1])
        rel_f = sb("rel_f", [BLOCKS, 1])
        row_f = sb("row_f", [BLOCKS, 1])
        steer = sb("steer", [BLOCKS, 2])
        table = sb("table", [2, BLOCKS], I32)
        pad = sb("pad", [P, ROW])
        xb = sb("xb", [P, RING, ROW])
        xbT = sb("xbT", [P, 3, P])
        gate = sb("gate", [P, 2, F])
        hid = sb("hid", [P, 3, F])
        WB = sb("WB", [P, 2, 2 * F])
        yb = sb("yb", [P, RING, P])
        y1 = sb("y1", [P, NT, P])
        y2 = sb("y2", [P, NT, P])

        ps = ctx.enter_context(nc.psum_tensor("ps", [P, 8, 512], F32))
        bank = lambda n: ps[:, n, :]
        ps_cqk = bank(BANK_CQK).rearrange("p (a n) -> p a n", a=2)
        ps_cv = bank(BANK_CV)[:, 0:T * P].rearrange("p (t c) -> p t c", t=T)
        ps_sim = bank(BANK_SIM).rearrange("p (t n) -> p t n", t=T)
        ps_pT = bank(BANK_PT).rearrange("p (k m) -> p k m", k=T)
        ps_co = bank(BANK_CO)[:, 0:T * P].rearrange("p (t c) -> p t c", t=T)
        ps_xT = bank(BANK_XT)[:, 0:N]
        ps_qk = bank(BANK_QK).rearrange("p (a n) -> p a n", a=2)
        ps_v = bank(BANK_V)[:, 0:T * P].rearrange("p (t c) -> p t c", t=T)
        ps_sc = bank(BANK_SC)[:, 0:B * T * H].rearrange("p (j g) -> p j g", j=B)
        ps_aT = bank(BANK_AT)[:, 0:N]
        ps_y = bank(BANK_Y)[:, 0:T * P].rearrange("p (t c) -> p t c", t=T)
        ps_x2T = bank(BANK_X2T)[:, 0:N]
        ps_log = bank(BANK_LOG)[:, 0:T * E].rearrange("p (t e) -> p t e", t=T)
        ps_rank = bank(BANK_RANK)[:, 0:T * E].rearrange("p (t e) -> p t e", t=T)
        ps_cnt = bank(7)[:, N + 2 * T * E:N + 2 * T * E + E]
        ps_table = bank(7)[0:2, N + 2 * T * E + E:N + 2 * T * E + E + BLOCKS]
        ps_xbT = bank(0)[:, 0:P]
        ps_yb = bank(2)[:, 0:P]
        ps_warm = bank(5)[:, 0:2 * P]
        ps_gu = [bank(3 + n) for n in range(2)]

        ld_conv = sem("ld_conv")
        ld_x = [sem(f"ld_x{i}") for i in range(B)]
        ld_vec = sem("ld_vec")
        ld_bias = sem("ld_bias")
        ld_tri = sem("ld_tri")
        ld_dest = sem("ld_dest")
        ld_lin = sem("ld_lin")
        ld_cst = sem("ld_cst")
        ld_w13 = sem("ld_w13")
        bias_ready = sem("bias_ready")
        tri_ready = sem("tri_ready")
        cqb_ready = sem("cqb_ready")
        dest_ready = sem("dest_ready")
        pad_ready = sem("pad_ready")
        cqk_done = sem("cqk_done")
        cqk_read = sem("cqk_read")
        cv_done = sem("cv_done")
        cv_read = sem("cv_read")
        sim_done = sem("sim_done")
        max_done = sem("max_done")
        exp_done = sem("exp_done")
        pT_done = sem("pT_done")
        pT_read = sem("pT_read")
        co_done = sem("co_done")
        t1_done = sem("t1_done")
        ve1_done = sem("ve1_done")
        rs1_done = sem("rs1_done")
        xn_done = sem("xn_done")
        xT_done = sem("xT_done")
        xT_read = sem("xT_read")
        lqk_done = sem("lqk_done")
        lqk_read = sem("lqk_read")
        lv_done = sem("lv_done")
        lv_read = sem("lv_read")
        qk_done = sem("qk_done")
        qkv_done = sem("qkv_done")
        sc_done = sem("sc_done")
        sco_done = sem("sco_done")
        num_done = sem("num_done")
        aT_done = sem("aT_done")
        aT_read = sem("aT_read")
        y_done = sem("y_done")
        t2_done = sem("t2_done")
        gsc_done = sem("gsc_done")
        ve2_done = sem("ve2_done")
        rs2_done = sem("rs2_done")
        xrow_done = sem("xrow_done")
        x2T_done = sem("x2T_done")
        x2T_read = sem("x2T_read")
        log_done = sem("log_done")
        gap_done = sem("gap_done")
        eg_done = sem("eg_done")
        w_done = sem("w_done")
        hits_done = sem("hits_done")
        rank_done = sem("rank_done")
        slot_done = sem("slot_done")
        scattered = sem("scattered")
        cnt_done = sem("cnt_done")
        pad_row_done = sem("pad_row_done")
        steer_done = sem("steer_done")
        table_turned = sem("table_turned")
        table_done = sem("table_done")
        pads_stored = sem("pads_stored")
        rinv_done = sem("rinv_done")
        den_done = sem("den_done")
        denm_done = sem("denm_done")
        dinv_done = sem("dinv_done")
        eg1_done = sem("eg1_done")
        wfirst_done = sem("wfirst_done")
        mask_done = sem("mask_done")
        base_done = sem("base_done")
        where_done = sem("where_done")
        st1_done = sem("st1_done")
        mv1_done = sem("mv1_done")
        st2_done = sem("st2_done")
        mv2_done = sem("mv2_done")
        top_done = sem("top_done")
        topi_done = sem("topi_done")
        dve = sem("dve")
        xb_loaded = [sem(f"xb_loaded{n}") for n in range(RING)]
        xbT_done = sem("xbT_done")
        xbT_read = sem("xbT_read")
        gu_done = sem("gu_done")
        gate_done = sem("gate_done")
        hid_done = sem("hid_done")
        wb_done = sem("wb_done")
        yb_done_pe = sem("yb_done_pe")
        yb_done = sem("yb_done")
        yb_stored = [sem(f"yb_stored{n}") for n in range(RING)]
        y1_loaded = [sem(f"y1_loaded{n}") for n in range(PARTS)]
        y2_loaded = [sem(f"y2_loaded{n}") for n in range(PARTS)]
        sum_done = sem("sum_done")
        out_stored = sem("out_stored")

        block = ctx.enter_context(nc.Block())
        rows_y_v = rows_y.rearrange("(c p t) d -> c p t d", c=TOP_K, p=P)

        def on_vector(i):
            return (i + 1) // VECTOR_SHARE

        def vector_shares(n):
            return sum(on_vector(i) > 0 for i in range(n))

        def nums(n):
            return sum(1 + i.bit_length() for i in range(n))

        def run_step(step, *stages):
            for stage, lag, *which in stages:
                if 0 <= step - lag < B:
                    stage(step - lag, *which)

        def pad_lists(eng, experts):
            eng.wait_ge(pad_row_done, 1)
            held = [eng.alloc_register(f"pad_row{e}") for e in experts]
            eng.reg_load(held, pad_row[0:1, experts[0]:experts[-1] + 1])
            for reg in held:
                row = eng.snap(reg, min_val=0, max_val=DUMMY - P)
                eng.dma_start(rows_x[bass.ds(row, P), :], pad[:, :]).then_inc(pads_stored, 16)

        def table_reader(eng, line, most):
            sets = [[eng.alloc_register(f"line{line}_{half}_{n}") for n in range(READ)] for half in range(2)]

            def read(s):
                held = sets[s // READ % 2]
                if s % READ == 0:
                    m = min(READ, BLOCKS - s)
                    eng.reg_load(held[0:m], table[line:line + 1, s:s + m])
                return eng.snap(held[s % READ], min_val=0, max_val=most)
            return read

        @block.sync
        def _(sp):
            sp.dma_start(X[:, 0, :], x_ch[:, 0, :]).then_inc(ld_x[0], 16)
            sp.dma_start(WC[:, :], w_conv).then_inc(ld_conv, 16)
            sp.dma_start(VEC[:, :], vecs).then_inc(ld_vec, 16)
            sp.dma_start(CF[:, :], cst_f).then_inc(ld_cst, 16)
            sp.dma_start(XT[:, 0, :, :], x_tok[:, 0, :, :]).then_inc(ld_x[0], 16)
            sp.dma_start(BR[:, :], bias_rows).then_inc(ld_bias, 16)
            sp.dma_start(WL[:, :], w_lin).then_inc(ld_lin, 16)
            sp.dma_start(WR[:, :], w_router).then_inc(ld_lin, 16)
            sp.dma_start(TRI32[:, :], cst_tri).then_inc(ld_tri, 16)
            sp.dma_start(DEST[:, :], cst_dest).then_inc(ld_dest, 16)
            for i in range(1, B):
                sp.dma_start(X[:, i, :], x_ch[:, i, :]).then_inc(ld_x[i], 16)
                sp.dma_start(XT[:, i, :, :], x_tok[:, i, :, :]).then_inc(ld_x[i], 16)
            sp.dma_start(W13[:, :], w13).then_inc(ld_w13, 16)
            sp.dma_start(W2[:, :], w2).then_inc(ld_w13, 16)

            sp.wait_ge(pad_ready, 2)
            sp.dma_start(rows_x[DUMMY:DUMMY + P, :], pad[:, :]).then_inc(pads_stored, 16)
            pad_lists(sp, range(0, E // 2))
            sp.wait_ge(table_done, 1)
            first_row = table_reader(sp, T_ROW, DUMMY)
            row = first_row(0)
            sp.wait_ge(pads_stored, 16 * (E + 1))
            sp.wait_ge(scattered, 16 * NT * TOP_K)
            for s in range(BLOCKS):
                if s >= RING:
                    sp.wait_ge(xbT_done, s - RING + 1)
                    sp.wait_ge(yb_stored[s % RING], 16 * (s // RING))
                sp.dma_start(xb[:, s % RING, :], rows_x[bass.ds(row, P), :]).then_inc(xb_loaded[s % RING], 16)
                if s + 1 < BLOCKS:
                    row = first_row(s + 1)

            for n in range(RING):
                sp.wait_ge(yb_stored[n], 16 * len(range(n, BLOCKS, RING)))
            for q in range(PARTS):
                a, b = q * NT // PARTS, (q + 1) * NT // PARTS
                sp.dma_start(y1[:, a:b, :], rows_y_v[0, :, a:b, :]).then_inc(y1_loaded[q], 16)
                sp.dma_start(y2[:, a:b, :], rows_y_v[1, :, a:b, :]).then_inc(y2_loaded[q], 16)
            for q in range(PARTS):
                a, b = q * NT // PARTS, (q + 1) * NT // PARTS
                sp.wait_ge(sum_done, q + 1)
                sp.dma_start(out[:, a:b, :], y2[:, a:b, :]).then_inc(out_stored, 16)
            sp.wait_ge(out_stored, 16 * PARTS)

        @block.gpsimd
        def _(pool):
            pool.memset(pad[:, 0:DEST_COL], 0.0).then_inc(pad_ready, 1)
            pool.memset(pad[:, DEST_COL:ROW].bitcast(I32), SKIP).then_inc(pad_ready, 1)
            pool.wait_ge(ld_dest, 16)
            pool.tensor_copy(xrow[:, :, :, DEST_COL].bitcast(I32).rearrange("p t c -> p (t c)"),
                             DEST[:, :]).then_inc(dest_ready, 1)

            def rstd_lin(i):
                pool.wait_ge(ve1_done, i + 1)
                if i >= 2:
                    pool.wait_ge(xn_done, 2 * (i - 1))
                pool.tensor_tensor(rs1[:, i % 2, :], ve1[:, i % 2, :], CF[:, C_HALF:C_HALF + T], ALU.pow).then_inc(rs1_done, 1)

            def rstd_ffn(i):
                pool.wait_ge(ve2_done, i + 1)
                if i >= 2:
                    pool.wait_ge(xrow_done, 2 * (i - 1))
                pool.tensor_tensor(rs2[:, i % 2, :], ve2[:, i % 2, :], CF[:, C_HALF:C_HALF + T], ALU.pow).then_inc(rs2_done, 1)

            def products(i):
                pool.wait_ge(lqk_read, 2 * (i + 1))
                if i >= 2:
                    pool.wait_ge(sc_done, i - 1)
                a = on_vector(i)
                pool.tensor_tensor(qk[:, i % 2, a:i + 1, :], kT[:, a:i + 1, :],
                                   qT[:, i % 2, :].unsqueeze(1).broadcast_to([P, i + 1 - a, N]), ALU.mult).then_inc(qk_done, 1)

            def scatter(i, t):
                pool.wait_ge(slot_done, i + 1)
                pool.wait_ge(w_done, 2 * (i + 1))
                pool.wait_ge(xrow_done, 2 * (i + 1))
                pool.wait_ge(dest_ready, 1)
                for c in range(TOP_K):
                    g = (i * T + t) * TOP_K + c
                    pool.indirect_dma_start(rows_x, bass.IndirectOffsetOnAxis(ap=slot[:, g:g + 1], axis=0),
                                            xrow[:, i * T + t, c, :], None, bounds_check=DUMMY + P - 1,
                                            oob_is_err=False).then_inc(scattered, 16)

            for step in range(STEPS):
                run_step(step, (scatter, 9, 0), (scatter, 9, 1), (rstd_lin, 2), (rstd_ffn, 6), (products, 3))

            last_row = pool.to_reg(TOP_K * TOKENS - 1)
            for s in range(BLOCKS):
                n = s % RING
                pool.wait_ge(yb_done, s + 1)
                pool.indirect_dma_start(
                    rows_y, bass.IndirectOffsetOnAxis(ap=xb[:, n, DEST_COL:ROW].bitcast(I32), axis=0),
                    yb[:, n, :], None, bounds_check=last_row, oob_is_err=False).then_inc(yb_stored[n], 16)

        @block.scalar
        def _(act):
            act.wait_ge(ld_vec, 16)
            act.mul(cqb8[:, :], VEC[0:PROJ + 1, V_CQB:V_CQB + 1], PROJ ** -0.5).then_inc(cqb_ready, 1)

            def conv_qk(i):
                b = i % 2
                act.wait_ge(cqk_done, i + 1)
                if i == 0:
                    act.wait_ge(cqb_ready, 1)
                if i >= 2:
                    act.wait_ge(sim_done, i - 1)
                act.activation(cq[:, b, :], ps_cqk[0:PROJ + 1, 0, :], ACT.Identity, bias=cqb8[:, :],
                               scale=PROJ ** -0.5).then_inc(cqk_read, 1)
                act.activation(ck[:, b, :], ps_cqk[0:PROJ + 1, 1, :], ACT.Identity,
                               bias=VEC[0:PROJ + 1, V_CKB:V_CKB + 1]).then_inc(cqk_read, 1)

            def conv_v(i):
                act.wait_ge(cv_done, i + 1)
                if i >= 2:
                    act.wait_ge(co_done, i - 1)
                act.activation(cv[:, i % 2, :, :], ps_cv, ACT.Copy).then_inc(cv_read, 1)

            def conv_exp(i):
                b = i % 2
                act.wait_ge(max_done, i + 1)
                if i >= 2:
                    act.wait_ge(pT_done, i - 1)
                    act.wait_ge(gsc_done, i - 1)
                for t in range(T):
                    act.activation(prob[:, b, t, :], ps_sim[:, t, :], ACT.Exp, bias=nmax[:, b, t:t + 1],
                                   accum_out=rsum[:, b, t:t + 1]).then_inc(exp_done, 1)

            def conv_pT(i):
                act.wait_ge(pT_done, i + 1)
                if i >= 2:
                    act.wait_ge(co_done, i - 1)
                act.activation(probT[:, i % 2, :, :], ps_pT, ACT.Copy).then_inc(pT_read, 1)

            def lin_xT(i):
                act.wait_ge(xT_done, i + 1)
                if i >= 2:
                    act.wait_ge(lv_done, i - 1)
                act.activation(xnT[:, i % 2, :], ps_xT, ACT.Copy).then_inc(xT_read, 1)

            def lin_qk(i):
                act.wait_ge(lqk_done, i + 1)
                if i >= 2:
                    act.wait_ge(qk_done, i - 1)
                if vector_shares(max(i - 1, 0)) > 0:
                    act.wait_ge(qkv_done, vector_shares(i - 1))
                act.activation(qT[:, i % 2, :], ps_qk[:, 0, :], ACT.Relu, bias=VEC[:, V_QB:V_QB + 1]).then_inc(lqk_read, 1)
                act.activation(kT[:, i, :], ps_qk[:, 1, :], ACT.Relu, bias=VEC[:, V_KB:V_KB + 1]).then_inc(lqk_read, 1)

            def lin_v(i):
                act.wait_ge(lv_done, i + 1)
                act.activation(vt[:, i, :].rearrange("p (t c) -> p t c", t=T), ps_v, ACT.Copy).then_inc(lv_read, 1)

            def lin_aT(i):
                act.wait_ge(aT_done, i + 1)
                if i >= 2:
                    act.wait_ge(y_done, i - 1)
                act.activation(attT[:, i % 2, :], ps_aT, ACT.Copy).then_inc(aT_read, 1)

            def route_xT(i):
                act.wait_ge(x2T_done, i + 1)
                if i >= 2:
                    act.wait_ge(log_done, i - 1)
                act.activation(x2T[:, i % 2, :], ps_x2T, ACT.Copy).then_inc(x2T_read, 1)

            def route_exp(i):
                act.wait_ge(gap_done, i + 1)
                if i >= 2:
                    act.wait_ge(w_done, 2 * (i - 1))
                act.activation(eg[:, i % 2, :], gap[:, i % 2, :], ACT.Exp).then_inc(eg_done, 1)

            for step in range(STEPS):
                run_step(step, (route_xT, 8), (conv_qk, 1), (lin_qk, 4), (conv_v, 1), (lin_v, 5), (lin_aT, 6), (conv_pT, 2),
                         (lin_xT, 3), (route_exp, 8), (conv_exp, 1))

            act.activation(warm[:, :], cqb8[:, :], ACT.Silu)
            act.wait_ge(pad_ready, 2)
            pad_lists(act, range(E // 2, E))

            def turned_x(s):
                act.wait_ge(xbT_done, s + 1)
                if s >= 3:
                    act.wait_ge(gu_done, s - 2)
                act.activation(xbT[:, s % 3, :], ps_xbT, ACT.Copy).then_inc(xbT_read, 1)

            def silu(s):
                act.wait_ge(gu_done, s + 1)
                if s >= 2:
                    act.wait_ge(hid_done, s - 1)
                act.activation(gate[:, s % 2, :], ps_gu[s % 2][:, 0:F], ACT.Silu).then_inc(gate_done, 1)

            for s in range(-2, BLOCKS):
                if s + 2 < BLOCKS:
                    turned_x(s + 2)
                if 0 <= s + 1 < BLOCKS:
                    silu(s + 1)

        @block.tensor
        def _(pe):
            bank_users = {}

            def bank_free(bank_number, read, count):
                if bank_number in bank_users:
                    pe.wait_ge(*bank_users[bank_number])
                bank_users[bank_number] = (read, count)

            def conv_proj_qk(i):
                if i == 0:
                    pe.wait_ge(ld_conv, 16)
                pe.wait_ge(ld_x[i], 32)
                bank_free(BANK_CQK, cqk_read, 2 * (i + 1))
                pe.matmul(ps_cqk[0:PROJ + 1, 0, :], wq, X[:, i, :], start=True, stop=True)
                pe.matmul(ps_cqk[0:PROJ + 1, 1, :], wk, X[:, i, :], start=True, stop=True).then_inc(cqk_done, 1)

            def conv_proj_v(i):
                pe.wait_ge(ld_x[i], 32)
                bank_free(BANK_CV, cv_read, i + 1)
                for t in range(T):
                    last = pe.matmul(ps_cv[:, t, :], X[:, i, t * P:(t + 1) * P], wv, start=True, stop=True)
                last.then_inc(cv_done, 1)

            def conv_scores(i):
                b = i % 2
                pe.wait_ge(cqk_read, 2 * (i + 1))
                bank_free(BANK_SIM, exp_done, 2 * (i + 1))
                for t in range(T):
                    last = pe.matmul(ps_sim[:, t, :], cq[:, b, t * P:(t + 1) * P], ck[:, b, :], start=True, stop=True)
                last.then_inc(sim_done, 1)

            def conv_turn(i):
                if i == 0:
                    pe.wait_ge(ld_cst, 16)
                pe.wait_ge(exp_done, 2 * (i + 1))
                bank_free(BANK_PT, pT_read, i + 1)
                for k in range(T):
                    for t in range(T):
                        last = pe.transpose(ps_pT[:, k, t * P:(t + 1) * P], prob[:, i % 2, t, k * P:(k + 1) * P], ident)
                last.then_inc(pT_done, 1)

            def conv_out(i):
                b = i % 2
                pe.wait_ge(pT_read, i + 1)
                pe.wait_ge(cv_read, i + 1)
                bank_free(BANK_CO, t1_done, 2 * (i + 1))
                for t in range(T):
                    for k in range(T):
                        last = pe.matmul(ps_co[:, t, :], probT[:, b, k, t * P:(t + 1) * P], cv[:, b, k, :],
                                         start=(k == 0), stop=(k == T - 1))
                last.then_inc(co_done, 1)

            def lin_turn(i):
                pe.wait_ge(xn_done, 2 * (i + 1))
                bank_free(BANK_XT, xT_read, i + 1)
                for t in range(T):
                    last = pe.transpose(ps_xT[:, t * P:(t + 1) * P], xn[:, i % 2, t, :], ident)
                last.then_inc(xT_done, 1)

            def lin_proj_qk(i):
                if i == 0:
                    pe.wait_ge(ld_lin, 32)
                    pe.wait_ge(bias_ready, 1)
                pe.wait_ge(xT_read, i + 1)
                bank_free(BANK_QK, lqk_read, 2 * (i + 1))
                pe.matmul(ps_qk[:, 0, :], lq, xnT[:, i % 2, :], start=True, stop=True)
                pe.matmul(ps_qk[:, 1, :], lk, xnT[:, i % 2, :], start=True, stop=True).then_inc(lqk_done, 1)

            def lin_proj_v(i):
                pe.wait_ge(xT_read, i + 1)
                bank_free(BANK_V, lv_read, i + 1)
                for t in range(T):
                    pe.matmul(ps_v[:, t, :], xnT[:, i % 2, t * P:(t + 1) * P], lv, start=True, stop=False)
                    last = pe.matmul(ps_v[:, t, :], ONES[:, :], vb_row, start=False, stop=True)
                last.then_inc(lv_done, 1)

            def lin_scores(i, share):
                first, end = ((0, on_vector(i)), (on_vector(i), i + 1))[share]
                if first == end:
                    return
                if share == 0:
                    pe.wait_ge(qkv_done, vector_shares(i + 1))
                else:
                    pe.wait_ge(qk_done, i + 1)
                if i >= 1:
                    pe.wait_ge(sco_done, i)
                for j in range(first, end):
                    heads = CF[:, C_COS + (i - j) * H:C_COS + (i - j + 1) * H]
                    for t in range(T):
                        last = pe.matmul(ps_sc[:, j, t * H:(t + 1) * H], qk[:, i % 2, j, t * P:(t + 1) * P], heads,
                                         start=True, stop=True)
                if share == 1:
                    last.then_inc(sc_done, 1)

            def lin_out_turn(i):
                pe.wait_ge(num_done, nums(i + 1))
                bank_free(BANK_AT, aT_read, i + 1)
                for t in range(T):
                    last = pe.transpose(ps_aT[:, t * P:(t + 1) * P], num[:, i % 2, 0, t * P:(t + 1) * P], ident)
                last.then_inc(aT_done, 1)

            def lin_out(i):
                pe.wait_ge(aT_read, i + 1)
                bank_free(BANK_Y, t2_done, i + 1)
                for t in range(T):
                    pe.matmul(ps_y[:, t, :], attT[:, i % 2, t * P:(t + 1) * P], lo, start=True, stop=False)
                    last = pe.matmul(ps_y[:, t, :], ONES[:, :], ob_row, start=False, stop=True)
                last.then_inc(y_done, 1)

            def route_turn(i):
                pe.wait_ge(xrow_done, 2 * (i + 1))
                bank_free(BANK_X2T, x2T_read, i + 1)
                for t in range(T):
                    last = pe.transpose(ps_x2T[:, t * P:(t + 1) * P], xrow[:, i * T + t, 0, 0:P], ident)
                last.then_inc(x2T_done, 1)

            def route_logits(i):
                pe.wait_ge(x2T_read, i + 1)
                bank_free(BANK_LOG, topi_done, 2 * (i + 1))
                for t in range(T):
                    last = pe.matmul(ps_log[:, t, :], x2T[:, i % 2, t * P:(t + 1) * P], WR[:, :], start=True, stop=True)
                last.then_inc(log_done, 1)

            def route_rank(i):
                pe.wait_ge(hits_done, 3 * (i + 1))
                bank_free(BANK_RANK, base_done, i + 1)
                pe.wait_ge(tri_ready, 1)
                for t in range(T):
                    pe.matmul(ps_rank[:, t, :], TRI[:, 0:P], hits[:, i % 2, t, :], start=True, stop=False)
                    last = pe.matmul(ps_rank[:, t, :], TRI[:, P:2 * P], seen[:, i * T + t, :], start=False, stop=True)
                last.then_inc(rank_done, 1)

            for step in range(STEPS):
                run_step(step, (lin_proj_qk, 4), (lin_proj_v, 5), (route_rank, 9), (conv_proj_v, 1), (lin_out_turn, 6),
                         (conv_turn, 2), (conv_scores, 1), (route_logits, 8), (lin_out, 6), (lin_turn, 3), (conv_out, 2),
                         (lin_scores, 4, 0), (conv_proj_qk, 0), (lin_scores, 4, 1), (route_turn, 7))

            pe.wait_ge(slot_done, B)
            pe.matmul(ps_cnt, TRI[:, P:2 * P], seen[:, NT, :], start=True, stop=True).then_inc(cnt_done, 1)
            pe.wait_ge(steer_done, 2)
            pe.transpose(ps_table, steer[:, :], CF[0:BLOCKS, C_ID:C_ID + BLOCKS]).then_inc(table_turned, 1)

            def turn_x(s):
                if s >= 1:
                    pe.wait_ge(xbT_read, s)
                pe.wait_ge(xb_loaded[s % RING], 16 * (s // RING + 1))
                pe.transpose(ps_xbT, xb[:, s % RING, 0:P], ident).then_inc(xbT_done, 1)

            def gate_up(s, e):
                if s >= 2:
                    pe.wait_ge(hid_done, s - 1)
                pe.wait_ge(xbT_read, s + 1)
                pe.wait_ge(wb_done, s + 1)
                for k in range(2 * FK):
                    last = pe.matmul(ps_gu[s % 2][:, k * P:(k + 1) * P], WB[:, s % 2, k * P:(k + 1) * P], xbT[:, s % 3, :],
                                     start=True, stop=True)
                last.then_inc(gu_done, 1)

            def down(s, e):
                if s >= 1:
                    pe.wait_ge(yb_done, s)
                pe.wait_ge(hid_done, s + 1)
                for k in range(FK):
                    last = pe.matmul(ps_yb, hid[:, s % 3, k * P:(k + 1) * P], W2[:, bass.ds(e * (FK * P) + k * P, P)],
                                     start=(k == 0), stop=(k == FK - 1))
                last.then_inc(yb_done_pe, 1)

            pe.wait_ge(ld_w13, 32)
            pe.wait_ge(table_done, 1)
            pe.wait_ge(pads_stored, 16 * (E + 1))
            for _ in range(WARM_MATMULS):
                pe.matmul(ps_warm, TRI[:, 0:P], TRI[:, :], start=True, stop=True)
            expert = table_reader(pe, T_EXPERT, E - 1)
            experts = [expert(0)]
            for s in range(-2, BLOCKS + 1):
                if s + 2 < BLOCKS:
                    turn_x(s + 2)
                if 0 <= s + 1 < BLOCKS:
                    gate_up(s + 1, experts[s + 1])
                    if s + 2 < BLOCKS:
                        experts.append(expert(s + 2))
                if 0 <= s - 1:
                    down(s - 1, experts[s - 1])

        @block.vector
        def _(dv):
            links = [0]

            def link(ins):
                links[0] += 1
                ins.then_inc(dve, 1)
                dv.wait_ge(dve, links[0])

            dv.memset(ONES[:, :], 1.0)
            link(dv.memset(BIAS[:, :], 0.0))
            dv.memset(seen[:, 0, :], 0.0)
            dv.memset(one8[:, :], 1.0)
            dv.wait_ge(ld_bias, 16)
            link(dv.tensor_copy(b_part[0][:, :], BR[:, :]))
            link(dv.tensor_tensor(b_rest[0][:, :], BR[:, :], b_part[0][:, :], ALU.subtract))
            link(dv.tensor_copy(b_part[1][:, :], b_rest[0][:, :]))
            link(dv.tensor_tensor(b_rest[1][:, :], b_rest[0][:, :], b_part[1][:, :], ALU.subtract))
            link(dv.tensor_copy(b_part[2][:, :], b_rest[1][:, :]))
            for n in range(3):
                last = dv.tensor_copy(BIAS[32 * n:32 * n + 1, :], b_part[n][32 * n:32 * n + 1, :])
                if n < 2:
                    link(last)
            last.then_inc(bias_ready, 1)
            dv.wait_ge(ld_tri, 16)
            dv.tensor_copy(TRI[:, :], TRI32[:, :]).then_inc(tri_ready, 1)
            dv.wait_ge(ld_vec, 16)
            dv.wait_ge(ld_cst, 16)

            def conv_max(i):
                dv.wait_ge(sim_done, i + 1)
                if i >= 2:
                    dv.wait_ge(exp_done, 2 * (i - 1))
                dv.tensor_reduce(nmax[:, i % 2, :], ps_sim, AX.X, ALU.max, negate=True).then_inc(max_done, 1)

            def conv_inverse(i):
                dv.wait_ge(exp_done, 2 * (i + 1))
                dv.reciprocal(rinv[:, i % 2, :], rsum[:, i % 2, :]).then_inc(rinv_done, 1)

            def conv_scale(i):
                dv.wait_ge(rinv_done, i + 1)
                dv.tensor_scalar(gsc[:, i % 2, :], rinv[:, i % 2, :], VEC[:, V_GAMMA:V_GAMMA + 1], None, ALU.mult)\
                  .then_inc(gsc_done, 1)

            def conv_add(i):
                dv.wait_ge(co_done, i + 1)
                dv.wait_ge(ld_x[i], 32)
                dv.wait_ge(gsc_done, i + 1)
                for t in range(T):
                    dv.scalar_tensor_tensor(out=t1[:, i, t, :], in0=ps_co[:, t, :], scalar=gsc[:, i % 2, t:t + 1],
                                            in1=XT[:, i, t, :], op0=ALU.mult, op1=ALU.add).then_inc(t1_done, 1)

            def lin_stats(i):
                dv.wait_ge(t1_done, 2 * (i + 1))
                for t in range(T):
                    dv.bn_stats(st1[:, i % 2, t, :], t1[:, i, t, :]).then_inc(st1_done, 1)

            def lin_moments(i):
                dv.wait_ge(st1_done, 2 * (i + 1))
                if i >= 2:
                    dv.wait_ge(xn_done, 2 * (i - 1))
                for t in range(T):
                    dv.bn_aggr(mv1[:, i % 2, t, :], st1[:, i % 2, t, :]).then_inc(mv1_done, 1)

            def lin_eps(i):
                dv.wait_ge(mv1_done, 2 * (i + 1))
                if i >= 2:
                    dv.wait_ge(rs1_done, i - 1)
                dv.tensor_scalar(ve1[:, i % 2, :], mv1[:, i % 2, :, 1], LN_EPS, None, ALU.add).then_inc(ve1_done, 1)

            def lin_norm(i):
                dv.wait_ge(rs1_done, i + 1)
                if i >= 2:
                    dv.wait_ge(xT_done, i - 1)
                for t in range(T):
                    dv.tensor_scalar(xn[:, i % 2, t, :], t1[:, i, t, :], mv1[:, i % 2, t, 0:1],
                                     rs1[:, i % 2, t:t + 1], ALU.subtract, ALU.mult).then_inc(xn_done, 1)

            def lin_products(i):
                a = on_vector(i)
                if a > 0:
                    dv.wait_ge(lqk_read, 2 * (i + 1))
                    dv.wait_ge(sc_done, i - 1)
                    dv.tensor_tensor(qk[:, i % 2, 0:a, :], kT[:, 0:a, :],
                                     qT[:, i % 2, :].unsqueeze(1).broadcast_to([P, a, N]), ALU.mult)\
                      .then_inc(qkv_done, 1)

            def lin_sum(i):
                dv.wait_ge(sc_done, i + 1)
                dv.tensor_reduce(den[:, i % 2, :], ps_sc[:, 0:i + 1, :].rearrange("p j g -> p g j"), AX.X, ALU.add)\
                  .then_inc(den_done, 1)

            def lin_floor(i):
                dv.wait_ge(den_done, i + 1)
                dv.tensor_scalar(denm[:, i % 2, :], den[:, i % 2, :], DEN_EPS, None, ALU.max).then_inc(denm_done, 1)

            def lin_inverse(i):
                dv.wait_ge(denm_done, i + 1)
                dv.reciprocal(dinv[:, i % 2, :], denm[:, i % 2, :]).then_inc(dinv_done, 1)

            def lin_weights(i):
                dv.wait_ge(dinv_done, i + 1)
                if i >= 2:
                    dv.wait_ge(num_done, nums(i - 1))
                dv.tensor_tensor(sco[:, i % 2, 0:i + 1, :], ps_sc[:, 0:i + 1, :],
                                 dinv[:, i % 2, :].unsqueeze(1).broadcast_to([P, i + 1, T * H]),
                                 ALU.mult).then_inc(sco_done, 1)

            def lin_values(i):
                dv.wait_ge(sco_done, i + 1)
                dv.wait_ge(lv_read, i + 1)
                if i >= 2:
                    dv.wait_ge(aT_done, i - 1)
                m, b = i + 1, i % 2
                w = sco[:, b, 0:m, :].rearrange("p j g -> p (j g)").unsqueeze(2).broadcast_to([P, m * T * H, D])
                dv.tensor_tensor(num[:, b, 0:m, :].rearrange("p j (g d) -> p (j g) d", d=D),
                                 vt[:, 0:m, :].rearrange("p j (g d) -> p (j g) d", d=D), w, ALU.mult)\
                  .then_inc(num_done, 1)

            def lin_fold(i, level):
                m = i + 1
                for _ in range(level):
                    m -= m // 2
                half = m // 2
                if half > 0:
                    b = i % 2
                    dv.wait_ge(num_done, nums(i) + 1 + level)
                    dv.tensor_tensor(num[:, b, 0:half, :], num[:, b, 0:half, :], num[:, b, m - half:m, :], ALU.add)\
                      .then_inc(num_done, 1)

            def lin_add(i):
                dv.wait_ge(y_done, i + 1)
                dv.tensor_tensor(t2[:, i * T:(i + 1) * T, :], ps_y, t1[:, i, :, :], ALU.add).then_inc(t2_done, 1)

            def route_stats(i):
                dv.wait_ge(t2_done, i + 1)
                for t in range(T):
                    dv.bn_stats(st2[:, i % 2, t, :], t2[:, i * T + t, :]).then_inc(st2_done, 1)

            def route_moments(i):
                dv.wait_ge(st2_done, 2 * (i + 1))
                if i >= 2:
                    dv.wait_ge(xrow_done, 2 * (i - 1))
                for t in range(T):
                    dv.bn_aggr(mv2[:, i % 2, t, :], st2[:, i % 2, t, :]).then_inc(mv2_done, 1)

            def route_eps(i):
                dv.wait_ge(mv2_done, 2 * (i + 1))
                if i >= 2:
                    dv.wait_ge(rs2_done, i - 1)
                dv.tensor_scalar(ve2[:, i % 2, :], mv2[:, i % 2, :, 1], LN_EPS, None, ALU.add).then_inc(ve2_done, 1)

            def route_norm(i):
                dv.wait_ge(rs2_done, i + 1)
                for t in range(T):
                    dv.tensor_scalar(xrow[:, i * T + t, :, 0:P],
                                     t2[:, i * T + t, :].unsqueeze(1).broadcast_to([P, TOP_K, P]),
                                     mv2[:, i % 2, t, 0:1], rs2[:, i % 2, t:t + 1], ALU.subtract, ALU.mult)\
                      .then_inc(xrow_done, 1)

            def route_top(i):
                dv.wait_ge(log_done, i + 1)
                for t in range(T):
                    dv.max(top[:, i % 2, t, :], ps_log[:, t, :]).then_inc(top_done, 1)

            def route_index(i):
                dv.wait_ge(top_done, 2 * (i + 1))
                for t in range(T):
                    dv.max_index(topi[:, i % 2, t, :], top[:, i % 2, t, :], ps_log[:, t, :]).then_inc(topi_done, 1)
                if i >= 2:
                    dv.wait_ge(eg_done, i - 1)
                dv.tensor_tensor(gap[:, i % 2, :], top[:, i % 2, :, 1], top[:, i % 2, :, 0], ALU.subtract)\
                  .then_inc(gap_done, 1)

            def route_mask(i):
                dv.wait_ge(topi_done, 2 * (i + 1))
                shape = [P, T, TOP_K, E]
                dv.tensor_tensor(mask[:, i % 2, :, :].rearrange("p (t c) e -> p t c e", c=TOP_K),
                                 CF[:, C_EXPERT:C_EXPERT + E].unsqueeze(1).unsqueeze(1).broadcast_to(shape),
                                 topi[:, i % 2, :, 0:TOP_K].unsqueeze(3).broadcast_to(shape), ALU.is_equal)\
                  .then_inc(mask_done, 1)

            def route_hits(i):
                dv.wait_ge(mask_done, i + 1)
                if i >= 2:
                    dv.wait_ge(rank_done, i - 1)
                m = mask[:, i % 2, :, :].rearrange("p (t c) e -> p t c e", c=TOP_K)
                dv.tensor_tensor(hits[:, i % 2, :, :], m[:, :, 0, :], m[:, :, 1, :], ALU.add).then_inc(hits_done, 1)

            def route_seen(i, t):
                dv.wait_ge(hits_done, 3 * i + 1 + t)
                n = i * T + t
                dv.tensor_tensor(seen[:, n + 1, :], seen[:, n, :], hits[:, i % 2, t, :], ALU.add)\
                  .then_inc(hits_done, 1)

            def route_sum(i):
                dv.wait_ge(eg_done, i + 1)
                dv.tensor_scalar(eg1[:, i % 2, :], eg[:, i % 2, :], 1.0, None, ALU.add).then_inc(eg1_done, 1)

            def route_first(i):
                dv.wait_ge(eg1_done, i + 1)
                dv.reciprocal(wfirst[:, i % 2, :], eg1[:, i % 2, :]).then_inc(wfirst_done, 1)

            def route_weights(i):
                dv.wait_ge(wfirst_done, i + 1)
                tiles = xrow[:, i * T:(i + 1) * T, :, :]
                dv.tensor_copy(tiles[:, :, 0, W_COL], wfirst[:, i % 2, :]).then_inc(w_done, 1)
                dv.tensor_tensor(tiles[:, :, 1, W_COL], eg[:, i % 2, :], wfirst[:, i % 2, :], ALU.mult).then_inc(w_done, 1)

            def route_base(i):
                dv.wait_ge(rank_done, i + 1)
                dv.tensor_tensor(base[:, i % 2, :, :], ps_rank,
                                 CF[:, C_ECAP:C_ECAP + E].unsqueeze(1).broadcast_to([P, T, E]), ALU.add)\
                  .then_inc(base_done, 1)

            def route_where(i):
                dv.wait_ge(base_done, i + 1)
                dv.tensor_tensor(where[:, i % 2, :, :].rearrange("p (t c) e -> p t c e", c=TOP_K),
                                 mask[:, i % 2, :, :].rearrange("p (t c) e -> p t c e", c=TOP_K),
                                 base[:, i % 2, :, :].unsqueeze(2).broadcast_to([P, T, TOP_K, E]), ALU.mult)\
                  .then_inc(where_done, 1)

            def route_slots(i):
                dv.wait_ge(where_done, i + 1)
                g = T * TOP_K
                with nc.allow_low_precision(reason="whole numbers below 2 ** 24, summed in float32"):
                    dv.tensor_reduce(slot[:, i * g:(i + 1) * g], where[:, i % 2, :, :], AX.X, ALU.add)\
                      .then_inc(slot_done, 1)

            for step in range(STEPS):
                run_step(step, (route_mask, 12), (lin_add, 10), (route_hits, 12), (conv_add, 6), (lin_fold, 9, 1), (lin_stats, 6),
                         (conv_inverse, 5), (route_stats, 10), (route_sum, 12), (route_seen, 12, 0), (lin_moments, 6),
                         (conv_scale, 5), (route_moments, 10), (route_seen, 12, 1), (lin_eps, 6), (route_first, 12),
                         (lin_fold, 9, 2), (lin_sum, 8), (route_eps, 10), (lin_floor, 8), (route_weights, 12),
                         (lin_inverse, 8), (lin_norm, 6), (lin_weights, 8), (route_base, 12), (lin_products, 7),
                         (route_where, 12), (lin_values, 8), (conv_max, 4), (route_slots, 12), (route_top, 11),
                         (route_norm, 10), (route_index, 11), (lin_fold, 8, 0))

            dv.wait_ge(cnt_done, 1)
            link(dv.tensor_copy(cnt[:, :], ps_cnt))
            dv.tensor_tensor(pad_row[:, :], cnt[0:1, :], CF[0:1, C_ECAP:C_ECAP + E], ALU.add).then_inc(pad_row_done, 1)
            link(dv.tensor_scalar(up[:, :], cnt[:, :], float(P - 1), None, ALU.add))
            link(dv.tensor_scalar(nbi[:, :], up[:, :], P.bit_length() - 1, None, ALU.logical_shift_right))
            link(dv.tensor_copy(nblk[:, :], nbi[:, :]))
            link(dv.tensor_tensor_scan(ends[:, :], one8[:, :], nblk[:, :], 0.0, ALU.mult, ALU.add))
            link(dv.tensor_scalar(past[:, :], ends[0:BLOCKS, :], CF[0:BLOCKS, C_TURN:C_TURN + 1], None, ALU.is_le))
            link(dv.tensor_tensor(skipped[:, :], past[:, :], nblk[0:BLOCKS, :], ALU.mult))
            link(dv.tensor_reduce(exp_f[:, :], past[:, :], AX.X, ALU.add))
            link(dv.tensor_reduce(first_f[:, :], skipped[:, :], AX.X, ALU.add))
            link(dv.tensor_scalar(rel_f[:, :], first_f[:, :], -float(P), CF[0:BLOCKS, C_TURN_ROW:C_TURN_ROW + 1],
                                  ALU.mult, ALU.add))
            link(dv.scalar_tensor_tensor(out=row_f[:, :], in0=exp_f[:, :], scalar=float(CAP), in1=rel_f[:, :],
                                         op0=ALU.mult, op1=ALU.add))
            dv.tensor_scalar(steer[:, T_ROW:T_ROW + 1], row_f[:, :], float(DUMMY), None, ALU.min).then_inc(steer_done, 1)
            dv.tensor_scalar(steer[:, T_EXPERT:T_EXPERT + 1], exp_f[:, :], float(E - 1), None, ALU.min)\
              .then_inc(steer_done, 1)
            dv.wait_ge(table_turned, 1)
            dv.tensor_copy(table[:, :], ps_table).then_inc(table_done, 1)

            def hidden(s):
                dv.wait_ge(gate_done, s + 1)
                if s >= 3:
                    dv.wait_ge(yb_done_pe, s - 2)
                dv.tensor_tensor(hid[:, s % 3, :], gate[:, s % 2, :], ps_gu[s % 2][:, F:2 * F], ALU.mult)\
                  .then_inc(hid_done, 1)

            def weights(s):
                if s >= 2:
                    dv.wait_ge(gu_done, s - 1)
                dv.tensor_copy(WB[:, s % 2, :], W13[:, bass.ds(experts[s] * (2 * F), 2 * F)]).then_inc(wb_done, 1)
                if s + 1 < BLOCKS:
                    experts.append(expert(s + 1))

            def weigh(s):
                n = s % RING
                dv.wait_ge(yb_done_pe, s + 1)
                if s >= RING:
                    dv.wait_ge(yb_stored[n], 16 * (s // RING))
                dv.tensor_scalar(yb[:, n, :], ps_yb, xb[:, n, W_COL:W_COL + 1], None, ALU.mult).then_inc(yb_done, 1)

            dv.wait_ge(ld_w13, 32)
            dv.wait_ge(table_done, 1)
            expert = table_reader(dv, T_EXPERT, E - 1)
            experts = [expert(0)]
            for s in range(-2, BLOCKS + 1):
                if s + 2 < BLOCKS:
                    weights(s + 2)
                if 0 <= s + 1 < BLOCKS:
                    hidden(s + 1)
                if s >= 1:
                    weigh(s - 1)

            for q in range(PARTS):
                a, b = q * NT // PARTS, (q + 1) * NT // PARTS
                dv.wait_ge(y1_loaded[q], 16)
                link(dv.tensor_tensor(y1[:, a:b, :], y1[:, a:b, :], t2[:, a:b, :], ALU.add))
                dv.wait_ge(y2_loaded[q], 16)
                dv.tensor_tensor(y2[:, a:b, :], y1[:, a:b, :], y2[:, a:b, :], ALU.add).then_inc(sum_done, 1)


def kernel(x, L0_conv_wq, L0_conv_bq, L0_conv_wk, L0_conv_bk, L0_conv_wv, L0_conv_wkm, L0_conv_bkm, L0_conv_gamma,
           L1_attn_q_w, L1_attn_q_b, L1_attn_k_w, L1_attn_k_b, L1_attn_v_w, L1_attn_v_b, L1_attn_out_w,
           L1_attn_out_b, L1_ffn_router_w, L1_ffn_w1, L1_ffn_w2, L1_ffn_w3):
    import concourse.bacc as bacc
    from concourse.bass_utils import run_bass_kernel_spmd

    x3 = np.asarray(x).reshape(B, P, N)
    zero_col = np.zeros((P, 1), np.float32)
    vecs = np.zeros((P, V_END), np.float32)
    vecs[:, V_QB], vecs[:, V_KB] = L1_attn_q_b, L1_attn_k_b
    vecs[0:PROJ, V_CQB], vecs[PROJ, V_CQB] = L0_conv_bq, PROJ ** 0.5
    vecs[0:PROJ, V_CKB], vecs[PROJ, V_CKB] = L0_conv_bk, L0_conv_bkm[0]
    vecs[:, V_GAMMA] = L0_conv_gamma[0]
    bias_rows = np.zeros((65, 2 * P), np.float32)
    bias_rows[::32] = np.concatenate([L1_attn_v_b, L1_attn_out_b])
    cst_f, cst_tri, cst_dest = constants()
    w13 = np.concatenate([L1_ffn_w1, L1_ffn_w3], axis=2)
    arrays = {
        "x_ch": x3.transpose(1, 0, 2),
        "x_tok": x3.reshape(B, P, T, P).transpose(3, 0, 2, 1),
        "w_conv": np.concatenate([np.asarray(L0_conv_wq).T, zero_col, np.asarray(L0_conv_wk).T,
                                  np.asarray(L0_conv_wkm).T, np.asarray(L0_conv_wv).T], axis=1),
        "w_lin": np.concatenate([np.asarray(w).T for w in (L1_attn_q_w, L1_attn_k_w, L1_attn_v_w, L1_attn_out_w)],
                                axis=1),
        "w_router": np.asarray(L1_ffn_router_w),
        "w13": w13.transpose(1, 0, 2).reshape(P, E * 2 * F),
        "w2": np.asarray(L1_ffn_w2).reshape(E, FK, P, P).transpose(2, 0, 1, 3).reshape(P, E * FK * P),
        "vecs": vecs,
        "bias_rows": bias_rows,
        "cst_f": cst_f,
        "cst_tri": cst_tri,
        "cst_dest": cst_dest,
    }
    arrays = {f"in_{n}": np.ascontiguousarray(a) for n, a in arrays.items()}
    nc = bacc.Bacc("TRN2", target_bir_lowering=False, num_devices=1)
    args = [nc.dram_tensor(n, a.shape, mybir.dt.from_np(a.dtype), kind="ExternalInput").ap()
            for n, a in arrays.items()]
    args.append(nc.dram_tensor("out_tok", (P, NT, P), F32, kind="ExternalOutput").ap())
    hybrid_block(nc, *args)
    r = run_bass_kernel_spmd(nc, [arrays], core_ids=[0])
    got = r.results[0]["out_tok"]
    return got.reshape(P, B, T, P).transpose(1, 3, 2, 0).reshape(B, P, 16, 16)
```
